# Optimizing a Trainium2 kernel written in Bass

```python
import numpy as np
import jax
import jax.numpy as jnp

def _softmax(x, axis=-1):
    return jax.nn.softmax(x, axis=axis)

def _gelu(x):
    return jax.nn.gelu(x, approximate=True)

def _silu(x):
    return jax.nn.silu(x)

def _sigmoid(x):
    return jax.nn.sigmoid(x)

def _layernorm(x, axis=-1, eps=1e-05):
    m = jnp.mean(x, axis=axis, keepdims=True)
    v = jnp.var(x, axis=axis, keepdims=True)
    return (x - m) / jnp.sqrt(v + eps)

def _scatter_add(tgt, idx, src, axis=0):
    return tgt.at[idx].add(src)

def _segment_sum(src, seg, n):
    return jax.ops.segment_sum(src, seg, n)
kernel_name = 'mk_audio_tower_d1_tok_audfeat2048_r4_0f15bf'

def setup_inputs(seed: int=0):
    np.random.seed(seed)
    _w = jnp.asarray

    def _rec_inputs():
        import jax
        import jax.numpy as jnp
        _rk = jax.random.key(seed)
        x = -0.000392918 + 0.999932 * jax.random.normal(jax.random.fold_in(_rk, 1), (64, 250, 64), jnp.float32)
        return x
    x = _rec_inputs()

    def _L0_tok_setup():
        import jax, jax.numpy as jnp
        import numpy as np
        TIN = 16
        FEAT = 64
        IN_DIM = TIN * FEAT
        HDIM = 512
        EPS = 1e-06

        def layer_norm(x, gamma, beta, eps):
            mu = jnp.mean(x, axis=-1, keepdims=True)
            var = jnp.mean(jnp.square(x - mu), axis=-1, keepdims=True)
            return (x - mu) * jax.lax.rsqrt(var + eps) * gamma + beta
        key = jax.random.key(seed)
        ks = jax.random.split(key, 4)
        x = jax.random.normal(ks[0], (64, 1024, FEAT), dtype=jnp.float32)
        W = jax.random.normal(ks[1], (IN_DIM, HDIM), dtype=jnp.float32) / np.sqrt(IN_DIM)
        b = jnp.zeros((HDIM,), dtype=jnp.float32)
        g1 = jnp.ones((IN_DIM,), dtype=jnp.float32)
        b1 = jnp.zeros((IN_DIM,), dtype=jnp.float32)
        g2 = jnp.ones((HDIM,), dtype=jnp.float32)
        b2 = jnp.zeros((HDIM,), dtype=jnp.float32)
        return {'x': x, 'W': W, 'b': b, 'g1': g1, 'b1': b1, 'g2': g2, 'b2': b2}
    _L0_tok_all = _L0_tok_setup()
    _L0_tok_in = {k: v for k, v in _L0_tok_all.items() if k in ('W', 'b', 'g1', 'b1', 'g2', 'b2')}
    del _L0_tok_all

    def _L0_attn_setup():
        import jax, jax.numpy as jnp
        import numpy as np
        B, T, C, H = (4, 1024, 512, 16)
        Dh = C // H

        def _feature_map(x):
            return jax.nn.elu(x) + 1.0
        key = jax.random.key(seed)
        ks = jax.random.split(key, 7)
        s = 0.02
        return {'x': jax.random.normal(ks[0], (B, T, C), dtype=jnp.float32), 'cos': jax.random.uniform(ks[1], (T, Dh), dtype=jnp.float32), 'sin': jax.random.uniform(ks[2], (T, Dh), dtype=jnp.float32), 'Wq': jax.random.normal(ks[3], (C, C), dtype=jnp.float32) * s, 'Wk': jax.random.normal(ks[4], (C, C), dtype=jnp.float32) * s, 'Wv': jax.random.normal(ks[5], (C, C), dtype=jnp.float32) * s, 'Wo': jax.random.normal(ks[6], (C, C), dtype=jnp.float32) * s}
    _L0_attn_all = _L0_attn_setup()
    _L0_attn_in = {k: v for k, v in _L0_attn_all.items() if k in ('cos', 'sin', 'Wq', 'Wk', 'Wv', 'Wo')}
    del _L0_attn_all

    def _L0_ffn_setup():
        import math
        import jax, jax.numpy as jnp
        import numpy as np
        NUM_EXPERTS = 8
        HIDDEN = 512
        INTER = 2048
        CAP_FACTOR = 1.25
        MIN_CAP = 4
        B, S = (4, 512)

        def _capacity(num_tokens: int, num_experts: int) -> int:
            cap = math.floor(CAP_FACTOR * num_tokens / num_experts)
            cap += cap % 2
            return max(cap, MIN_CAP)
        key = jax.random.key(seed)
        k1, k2, k3, k4 = jax.random.split(key, 4)
        std_h = math.sqrt(0.1 / HIDDEN)
        std_i = math.sqrt(0.1 / INTER)
        inputs = jax.random.normal(k1, (B, S, HIDDEN), dtype=jnp.float32)
        gate_weight = jax.random.normal(k2, (NUM_EXPERTS, HIDDEN), dtype=jnp.float32) * std_h
        wi = jax.random.normal(k3, (NUM_EXPERTS, HIDDEN, INTER), dtype=jnp.float32) * std_h
        wo = jax.random.normal(k4, (NUM_EXPERTS, INTER, HIDDEN), dtype=jnp.float32) * std_i
        return {'inputs': inputs, 'gate_weight': gate_weight, 'wi': wi, 'wo': wo}
    _L0_ffn_all = _L0_ffn_setup()
    _L0_ffn_in = {k: v for k, v in _L0_ffn_all.items() if k in ('gate_weight', 'wi', 'wo')}
    del _L0_ffn_all
    return {'x': x, 'L0_tok_W': _L0_tok_in['W'], 'L0_tok_b': _L0_tok_in['b'], 'L0_tok_g1': _L0_tok_in['g1'], 'L0_tok_b1': _L0_tok_in['b1'], 'L0_tok_g2': _L0_tok_in['g2'], 'L0_tok_b2': _L0_tok_in['b2'], 'L0_attn_cos': _L0_attn_in['cos'], 'L0_attn_sin': _L0_attn_in['sin'], 'L0_attn_Wq': _L0_attn_in['Wq'], 'L0_attn_Wk': _L0_attn_in['Wk'], 'L0_attn_Wv': _L0_attn_in['Wv'], 'L0_attn_Wo': _L0_attn_in['Wo'], 'L0_ffn_gate_weight': _L0_ffn_in['gate_weight'], 'L0_ffn_wi': _L0_ffn_in['wi'], 'L0_ffn_wo': _L0_ffn_in['wo']}

def reference(x, L0_tok_W, L0_tok_b, L0_tok_g1, L0_tok_b1, L0_tok_g2, L0_tok_b2, L0_attn_cos, L0_attn_sin, L0_attn_Wq, L0_attn_Wk, L0_attn_Wv, L0_attn_Wo, L0_ffn_gate_weight, L0_ffn_wi, L0_ffn_wo):
    import jax
    import jax.numpy as jnp

    def _L0_tok_ref(x, W, b, g1, b1, g2, b2):
        import jax, jax.numpy as jnp
        import numpy as np
        TIN = 16
        FEAT = 64
        IN_DIM = TIN * FEAT
        HDIM = 512
        EPS = 1e-06

        def layer_norm(x, gamma, beta, eps):
            mu = jnp.mean(x, axis=-1, keepdims=True)
            var = jnp.mean(jnp.square(x - mu), axis=-1, keepdims=True)
            return (x - mu) * jax.lax.rsqrt(var + eps) * gamma + beta
        bsz, T, F = x.shape
        n_patch = T // TIN
        x = x[:, :n_patch * TIN, :].reshape(bsz, n_patch, TIN * F)
        x = layer_norm(x, g1, b1, EPS)
        x = jnp.einsum('bpd,dh->bph', x, W) + b
        return layer_norm(x, g2, b2, EPS)

    def _L0_attn_ref(x, cos, sin, Wq, Wk, Wv, Wo):
        import jax, jax.numpy as jnp
        import numpy as np
        B, T, C, H = (4, 1024, 512, 16)
        Dh = C // H

        def _feature_map(x):
            return jax.nn.elu(x) + 1.0
        b, t, c = x.shape
        h, dh = (H, c // H)

        def proj(W):
            y = jnp.einsum('btc,oc->bto', x, W)
            return y.reshape(b, t, h, dh).transpose(0, 2, 1, 3)
        q = _feature_map(proj(Wq))
        k = _feature_map(proj(Wk))
        v = proj(Wv)
        kv = jnp.einsum('bhtd,bhte->bhde', k, v)
        z = 1.0 / (jnp.einsum('bhtd,bhd->bht', q, k.sum(axis=2)) + 1e-06)
        out = jnp.einsum('bhtd,bhde,bht->bhte', q, kv, z)
        out = out.transpose(0, 2, 1, 3).reshape(b, t, c)
        return jnp.einsum('btc,oc->bto', out, Wo)

    def _L0_ffn_ref(inputs, gate_weight, wi, wo):
        import math
        import jax, jax.numpy as jnp
        import numpy as np
        NUM_EXPERTS = 8
        HIDDEN = 512
        INTER = 2048
        CAP_FACTOR = 1.25
        MIN_CAP = 4
        B, S = (4, 512)

        def _capacity(num_tokens: int, num_experts: int) -> int:
            cap = math.floor(CAP_FACTOR * num_tokens / num_experts)
            cap += cap % 2
            return max(cap, MIN_CAP)
        b, s, h = inputs.shape
        tokens = inputs.reshape(-1, h)
        T = tokens.shape[0]
        E = gate_weight.shape[0]
        C = _capacity(T, E)
        logits = tokens.astype(jnp.float32) @ gate_weight.astype(jnp.float32).T
        probs = jax.nn.softmax(logits, axis=-1)
        top1 = jnp.argmax(logits, axis=-1)
        mask = jax.nn.one_hot(top1, E, dtype=jnp.int32)
        ranks = jnp.cumsum(mask, axis=0) - 1
        mask = mask * (ranks < C).astype(jnp.int32)
        ranks_tok = jnp.sum(mask * ranks, axis=-1)
        ranks_oh = jax.nn.one_hot(ranks_tok, C, dtype=jnp.float32)
        weight = mask.astype(probs.dtype) * probs
        combine_weights = weight[:, :, None] * ranks_oh[:, None, :]
        sec_mask = jax.lax.stop_gradient(combine_weights != 0).astype(inputs.dtype)
        dispatch = jnp.einsum('tec,th->ech', sec_mask, tokens)
        hmid = jnp.einsum('ech,ehi->eci', dispatch, wi)
        hmid = jax.nn.gelu(hmid, approximate=False)
        eout = jnp.einsum('eci,eih->ech', hmid, wo)
        out = jnp.einsum('tec,ech->th', combine_weights.astype(inputs.dtype), eout)
        return out.reshape(b, s, h)
    h = _L0_tok_ref(x, L0_tok_W, L0_tok_b, L0_tok_g1, L0_tok_b1, L0_tok_g2, L0_tok_b2)
    h = h + _L0_attn_ref(_layernorm(h, axis=-1), L0_attn_cos, L0_attn_sin, L0_attn_Wq, L0_attn_Wk, L0_attn_Wv, L0_attn_Wo)
    h = h + _L0_ffn_ref(_layernorm(h, axis=-1), L0_ffn_gate_weight, L0_ffn_wi, L0_ffn_wo)
    return h

_drawn_inputs = setup_inputs


def setup_inputs(seed=0):
    import zlib

    import numpy as np

    out = dict(_drawn_inputs(seed))
    spreads = {'L0_tok_b': (0.0, 0.1),
     'L0_tok_g1': (1.0, 0.2),
     'L0_tok_b1': (0.0, 0.1),
     'L0_tok_g2': (1.0, 0.2),
     'L0_tok_b2': (0.0, 0.1)}
    factors = {'L0_attn_Wq': 8.0,
     'L0_attn_Wk': 8.0,
     'L0_ffn_gate_weight': 5.888,
     'L0_ffn_wi': 5.443,
     'L0_ffn_wo': 5.294}
    for name, (base, spread) in spreads.items():
        noise = np.random.default_rng([zlib.crc32(name.encode()), seed]).standard_normal(out[name].shape)
        drawn = base * np.exp(spread * noise) if base else spread * noise
        out[name] = jnp.asarray(drawn.astype(out[name].dtype))
    for name, factor in factors.items():
        out[name] = (out[name] * factor).astype(out[name].dtype)
    return out
```

```python
from contextlib import ExitStack

import numpy as np
import concourse.bass as bass
from concourse import mybir

F32 = mybir.dt.float32
BF16 = mybir.dt.bfloat16
U32 = mybir.dt.uint32
ALU = mybir.AluOpType
ACT = mybir.ActivationFunctionType
AX_X = mybir.AxisListType.X

P = 128
BATCH, SEQ, FEAT = 64, 250, 64
TIN = 16
NPATCH = SEQ // TIN
IN_DIM = TIN * FEAT
C = 512
TOKENS = BATCH * NPATCH
BT = 8
TT = BT * NPATCH
NT = TOKENS // TT
HALF = NT // 2
HT = HALF * TT
KX = IN_DIM // P
KC = C // P
DH = 32
HPB = P // DH
E = 8
INTER = 2048
KI = INTER // P
CAP = TOKENS * 5 // 4 // E
CH = CAP // 2
EPS_TOK, EPS_LN, EPS_Z = 1e-6, 1e-5, 1e-6

PIECES = 8
WP = PIECES // 2
SLOTS = 2 * PIECES
EARLY = 5
SLOT_B = 4 * KC * C

XS_ROWS = (E + 2) * CAP
EO_ROWS = (E + 1) * CAP

CO_ID = 0
CO_BLK = CO_ID + P
CO_MASK = CO_BLK + P
CO_TRI = CO_MASK + TT
CO_ONE = CO_TRI + TT
CO_HM = CO_ONE + TT
CO_REV = CO_HM + HPB
CO_OFF = CO_REV + NT * E
CO_TOK = CO_OFF + NT * E
CO_N = CO_TOK + NT


def constants():
    c = np.zeros((P, CO_N), np.float32)
    r = np.arange(P)
    c[:, CO_ID:CO_ID + P] = np.eye(P)
    c[:, CO_BLK:CO_BLK + P] = r[:, None] // DH == r[None] // DH
    s = np.arange(TT)
    c[:TT, CO_MASK:CO_MASK + TT] = s[:, None] // NPATCH == s[None] // NPATCH
    c[:TT, CO_TRI:CO_TRI + TT] = s[:, None] < s[None]
    c[:TT, CO_ONE:CO_ONE + TT] = 1
    c[:, CO_HM:CO_HM + HPB] = r[:, None] // DH == np.arange(HPB)[None]
    c[:, CO_REV:CO_REV + NT * E] = np.tile(E - np.arange(E), NT)
    c[:, CO_OFF:CO_OFF + NT * E] = np.tile(CAP * np.arange(E), NT)
    c[:TT, CO_TOK:CO_TOK + NT] = XS_ROWS + s[:, None] + TT * np.arange(NT)[None]
    return c


def audio_tower(nc, x, w_tok, cols, g2b2b, wq, wk, wv, wo, gate, wi, wout, consts, out):
    xs_dram = nc.dram_tensor("xs_rows", (XS_ROWS + TOKENS, C), F32).ap()
    eo_dram = nc.dram_tensor("eo_rows", (EO_ROWS, C), F32).ap()

    with ExitStack() as ctx:
        def psum(name, shape):
            return ctx.enter_context(nc.psum_tensor(name, shape, F32))

        def sem(name):
            return ctx.enter_context(nc.semaphore(name))

        start = (nc.sbuf_base + 63) // 64 * 64
        size = (nc.sbuf_bytes_remaining - 128) // 64 * 64
        ctx.enter_context(nc.sbuf_tensor("arena", [P, size], mybir.dt.uint8))
        at = [start]

        def place(name, shape, dt=F32):
            n = int(np.prod(shape[1:])) * (2 if dt == BF16 else 4)
            t = nc.alloc_sbuf_tensor_at(name, shape, dt, offset=at[0])
            at[0] += (n + 31) // 32 * 32
            assert at[0] <= start + size, (name, at[0] - start - size)
            return t

        cst = place("cst", [P, CO_N])
        h2 = place("h2", [TT, NT, C])
        rows = place("rows", [TT, NT, C])
        logits = place("logits", [TT, NT, E])
        prob = place("prob", [TT, NT])
        src_idx = place("src_idx", [TT, NT], U32)
        ring = [place(f"ring{s}", [P, KC, C]) for s in range(EARLY)]
        shared = at[0]

        wtok = place("wtok", [P, KX, C])
        wqs, wks, wvs, wos = (place(n, [P, KC, C]) for n in ("wqs", "wks", "wvs", "wos"))
        vec = place("vec", [P, 2 * KX])
        bcst = place("bcst", [TT, 3, C])
        gsb = place("gsb", [P, KC, E])
        xt = place("xt", [TT, 2, IN_DIM])
        xT = place("xT", [P, 2, KX, TT])
        anT = place("anT", [P, KC, HT])
        qT = place("qT", [P, KC, HT])
        kT = place("kT", [P, KC, HT])
        vsb = place("vsb", [TT, HALF, C])
        ebuf = place("ebuf", [P, 2, HT])
        an = place("an", [TT, 2, C])
        qblk = place("qblk", [P, 2, HPB * TT])
        ssb = place("ssb", [TT, 2, HPB * TT])
        attT = place("attT", [P, 2, KC, TT])
        t2T = place("t2T", [P, 2, KC, TT])
        stats = place("stats", [TT, 4, 2, 6])
        mv = place("mv", [TT, 4, 4, 2])
        std = place("std", [TT, 4, 4])
        rstd = place("rstd", [TT, 4, 4])
        ksum = place("ksum", [P, KC, HT // NPATCH])

        at[0] = shared
        ring += [place(f"ring{s}", [P, KC, C]) for s in range(EARLY, SLOTS)]
        xrow = place("xrow", [CH, 2, 2, C])
        xTe = place("xTe", [P, 2, KC, CAP])
        hm_at = at[0]
        hmT = place("hmT", [P, 2, KI, CAP])
        eT = place("eT", [P, 2, KC, CAP])
        eorow = place("eorow", [CH, 2, 2, C])
        after, at[0] = at[0], hm_at + 4 * KI * CAP
        rt = place("rt", [TT, 8, NT * E])
        rs = place("rs", [TT, 8, NT])
        ohb = place("ohb", [TT, NT * E], BF16)
        trib = place("trib", [TT, 2 * TT], BF16)
        dst_idx = place("dst_idx", [TT, NT], U32)
        at[0] = after

        ident = cst[:, CO_ID:CO_ID + P]

        ps_x = psum("ps_x", [P, 2, 512])
        ps_p = psum("ps_p", [P, 2, 512])
        ps_t = psum("ps_t", [P, 512])
        ps_o = psum("ps_o", [P, 512])
        ps_s = psum("ps_s", [P, 2, 512])
        ps_h = [ps_x, ps_p]
        ps_e = [ps_t, ps_o]

        c_in, v_in, z_out, z_set = sem("c_in"), sem("v_in"), sem("z_out"), sem("z_set")
        wtok_in, wq_in, wk_in, wv_in, wo_in = (sem(f"w{n}_in") for n in ("tok", "q", "k", "v", "o"))
        x_in = [sem(f"x_in{u}") for u in range(2)]
        slot_in = [sem(f"slot_in{s}") for s in range(SLOTS)]
        scat, xrow_in, eo_out, gath, y_out = sem("scat"), [sem("xrow_in0"), sem("xrow_in1")], sem("eo_out"), sem("gath"), sem("y_out")
        bias_ps, bias_sb, w_scaled = sem("bias_ps"), sem("bias_sb"), sem("w_scaled")
        mv_rdy, std_rdy = sem("mv_rdy"), sem("std_rdy")
        x_norm, xT_ps, xT_sb, h_ps, h_evac, h_norm, h_mul, h_rdy = (sem(n) for n in (
            "x_norm", "xT_ps", "xT_sb", "h_ps", "h_evac", "h_norm", "h_mul", "h_rdy"))
        a_norm, aT_ps, aT_sb, v_ps, v_sb, qk_ps, e_sb, qk_sb = (sem(n) for n in (
            "a_norm", "aT_ps", "aT_sb", "v_ps", "v_sb", "qk_ps", "e_sb", "qk_sb"))
        qks_rdy, den_ps, qn_rdy, qb_rdy, s_ps, s_sb, n_ps, att_sb = (sem(n) for n in (
            "qks_rdy", "den_ps", "qn_rdy", "qb_rdy", "s_ps", "s_sb", "n_ps", "att_sb"))
        wo_ps, h2_rdy, t_norm, tT_ps, tT_sb, g_ps, lg_sb = (sem(n) for n in (
            "wo_ps", "h2_rdy", "t_norm", "tT_ps", "tT_sb", "g_ps", "lg_sb"))
        dve_step, waited = sem("dve_step"), sem("waited")
        r_diff, r_exp, r_oh, r_ps, idx_rdy = sem("r_diff"), sem("r_exp"), sem("r_oh"), sem("r_ps"), sem("idx_rdy")
        rows_rdy, eo_free = sem("rows_rdy"), sem("eo_free")
        rowT_ps, rowT_sb, hm_ps, g_sb, ew_ps, eT_rdy, oT_ps, eo_rdy, o_rdy = (sem(n) for n in (
            "rowT_ps", "rowT_sb", "hm_ps", "g_sb", "ew_ps", "eT_rdy", "oT_ps", "eo_rdy", "o_rdy"))

        block = ctx.enter_context(nc.Block())

        x_t = x.rearrange("(t p) d -> t p d", p=TT)
        out_t = out.rearrange("(t p) d -> t p d", p=TT)
        wi_v = wi.rearrange("(i q) (k p) (j n) -> i q j p k n", q=2, p=P, n=C)
        wo_v = wout.rearrange("(i q) (j k p) n -> i q j p k n", q=2, p=P, k=KC)
        xs_v = xs_dram[0:XS_ROWS].rearrange("(i q c p) d -> i q p c d", q=2, c=2, p=CH)
        eo_v = eo_dram.rearrange("(e c p) d -> e p c d", c=2, p=CH)

        order = []
        for s in range(HALF + 2):
            order += [(r, s - r) for r in range(3) if 0 <= s - r < HALF]
        order += [(3, u) for u in range(HALF)]

        class Steps:

            def __init__(self, eng, base):
                self.eng, self.base, self.n = eng, base, 0

            def done(self, ins, alone=False):
                self.n += 1
                ins.then_inc(dve_step, 1)
                (apart if alone else type(self.eng).wait_ge)(self.eng, dve_step, self.base + self.n)

        def apart(eng, sem_, value):
            eng.wait_ge(sem_, value)
            eng.sem_inc(waited, 1)

        @block.sync
        def _(sp):
            sp.dma_start(xt[:, 0], x_t[0]).then_inc(x_in[0], 16)
            sp.dma_start(cst[:], consts).then_inc(c_in, 16)
            sp.dma_start(vec[:], cols).then_inc(v_in, 16)
            sp.dma_start(bcst[:], g2b2b.partition_broadcast(TT)).then_inc(v_in, 16)
            sp.dma_start(gsb[:], gate.rearrange("(k p) e -> p k e", p=P)).then_inc(v_in, 16)
            sp.dma_start(wtok[:], w_tok.rearrange("(k p) n -> p k n", p=P)).then_inc(wtok_in, 16)
            sp.dma_start(xt[:, 1], x_t[1]).then_inc(x_in[1], 16)
            for w, to, s in ((wv, wvs, wv_in), (wq, wqs, wq_in), (wk, wks, wk_in), (wo, wos, wo_in)):
                sp.dma_start(to[:], w.rearrange("(k p) n -> p k n", p=P)).then_inc(s, 16)

            def piece(i, s):
                q, j = s // PIECES, s % PIECES
                src = wi_v[i, q, j] if j < WP else wo_v[i, q, j - WP]
                sp.dma_start(ring[s][:], src).then_inc(slot_in[s], 16)

            for s in range(2):
                piece(0, s)
            for t in range(2, NT):
                sp.wait_ge(xT_ps, t - 1)
                sp.dma_start(xt[:, t % 2], x_t[t]).then_inc(x_in[t % 2], 16)
                if t < EARLY:
                    piece(0, t)
            sp.wait_ge(lg_sb, NT)
            for s in range(EARLY, SLOTS):
                piece(0, s)
            with sp.Fori(1, E // 2) as i:
                for s in range(SLOTS):
                    q, j = s // PIECES, s % PIECES
                    used = hm_ps if j < WP else ew_ps
                    sp.wait_ge(used, 2 * WP * i + (q * WP + j % WP + 1 - 2 * WP))
                    piece(i, s)
            for t in range(NT):
                sp.wait_ge(o_rdy, t + 1)
                sp.dma_start(out_t[t], h2[:, t]).then_inc(y_out, 16)
            sp.wait_ge(y_out, 16 * NT)

        @block.gpsimd
        def _(pool):
            pool.wait_ge(c_in, 16)
            pool.wait_ge(v_in, 48)
            with pool.Fori(0, 2) as g:
                for u in range(HALF):
                    apart(pool, h_norm, HALF * g + u + 1)
                    hn = h2[:, HALF * g + u]
                    nc.gpsimd.tensor_tensor(hn, hn, bcst[:, 0], ALU.mult).then_inc(h_mul, 1)
                    apart(pool, h_mul, HALF * g + u + 1)
                    nc.gpsimd.tensor_tensor(hn, hn, bcst[:, 1], ALU.add).then_inc(h_rdy, 1)
                for n in range(HALF * KC):
                    u, m = n // KC, n % KC
                    if u == 0:
                        pool.wait_ge(qn_rdy, KC * g + m + 1)
                    if n >= 2:
                        pool.wait_ge(s_ps, HALF * KC * g + n - 1)
                    q4 = qT[:, m, u * TT:(u + 1) * TT].unsqueeze(1).to_broadcast([P, HPB, TT])
                    hm4 = cst[:, CO_HM:CO_HM + HPB].unsqueeze(2).to_broadcast([P, HPB, TT])
                    nc.gpsimd.tensor_tensor(qblk[:, n % 2].rearrange("p (h t) -> p h t", h=HPB),
                                            q4, hm4, ALU.mult).then_inc(qb_rdy, 1)
            pool.wait_ge(z_set, 1)
            z = hmT[0:CH, 0].rearrange("p k c -> p (k c)")[:, 0:2 * C]
            for e in range(E + 2):
                pool.dma_start(xs_v[e // 2, e % 2], z.rearrange("p (c d) -> p c d", c=2)).then_inc(z_out, 16)
            pool.wait_ge(z_out, 16 * (E + 2))
            pool.wait_ge(idx_rdy, 1)
            pool.wait_ge(rows_rdy, NT)
            for t in range(NT):
                pool.indirect_dma_start(
                    out=xs_dram, out_offset=bass.IndirectOffsetOnAxis(ap=dst_idx[:, t:t + 1], axis=0),
                    in_=rows[:, t], in_offset=None).then_inc(scat, 16)
            pool.wait_ge(scat, 16 * NT)
            for q in range(2):
                pool.dma_start(xrow[:, q], xs_v[0, q]).then_inc(xrow_in[q], 16)
            pool.sem_inc(eo_free, 2)
            with pool.Fori(0, E // 2) as i:
                for q in range(2):
                    pool.wait_ge(eo_rdy, 2 * i + q + 1)
                    pool.dma_start(eo_v[2 * i + q], eorow[:, 1 - q]).then_inc(eo_out, 16)
                    pool.wait_ge(rowT_ps, 2 * i + q + 1)
                    pool.dma_start(xrow[:, q], xs_v[i + 1, q]).then_inc(xrow_in[q], 16)
                    pool.wait_ge(eo_out, 32 * i + 16 * (q + 1))
                    pool.sem_inc(eo_free, 1)
            pool.wait_ge(eo_rdy, E + 1)
            pool.dma_start(eo_v[E], eorow[:, (E - 1) % 2]).then_inc(eo_out, 16)
            pool.wait_ge(eo_out, 16 * (E + 1))
            pool.wait_ge(xrow_in[0], 16 * (E // 2 + 1))
            pool.wait_ge(xrow_in[1], 16 * (E // 2 + 1))
            for t in range(NT):
                pool.indirect_dma_start(
                    out=rows[:, t], out_offset=None, in_=eo_dram,
                    in_offset=bass.IndirectOffsetOnAxis(ap=src_idx[:, t:t + 1], axis=0)).then_inc(gath, 16)
            pool.wait_ge(gath, 16 * NT)

        @block.scalar
        def _(act):
            act.wait_ge(bias_ps, 1)
            act.wait_ge(v_in, 48)
            for k in range(KX):
                nc.scalar.activation(wtok[:, k], wtok[:, k], ACT.Copy, scale=vec[:, k:k + 1]).then_inc(w_scaled, 1)

            def root(r, g, u, eps):
                act.wait_ge(mv_rdy, 4 * HALF * g + order.index((r, u)) + 1)
                nc.scalar.activation(std[:, r, u:u + 1], mv[:, r, u, 1:2], ACT.Sqrt).then_inc(std_rdy, 1)

            with act.Fori(0, 2) as g:
                for s in range(HALF + 3):
                    if s < HALF:
                        root(0, g, s, EPS_TOK)
                        act.wait_ge(xT_ps, HALF * g + s + 1)
                        if s >= 2:
                            act.wait_ge(h_ps, HALF * g + s - 1)
                        nc.scalar.activation(xT[:, s % 2].rearrange("p (b k) t -> p b (k t)", b=2),
                                             ps_x[:, :, 0:HT], ACT.Copy).then_inc(xT_sb, 1)
                    if 0 <= s - 1 < HALF:
                        root(1, g, s - 1, EPS_TOK)
                    if 0 <= s - 2 < HALF:
                        root(2, g, s - 2, EPS_LN)
                    if 0 <= s - 3 < HALF:
                        u = s - 3
                        act.wait_ge(aT_ps, HALF * g + u + 1)
                        nc.scalar.activation(anT[:, :, u * TT:(u + 1) * TT],
                                             ps_t[:, 0:HT].rearrange("p (k t) -> p k t", k=KC),
                                             ACT.Copy).then_inc(aT_sb, 1)
                for u in range(HALF):
                    act.wait_ge(v_ps, HALF * g + u + 1)
                    nc.scalar.activation(vsb[:, u], ps_p[0:TT, u % 2], ACT.Copy).then_inc(v_sb, 1)
                for j in range(2 * KC):
                    act.wait_ge(qk_ps, 2 * KC * g + j + 1)
                    if j >= 2:
                        act.wait_ge(qk_sb, 2 * KC * g + j - 1)
                    nc.scalar.activation(ebuf[:, j % 2], ps_p[:, j % 2, 0:HT], ACT.Exp).then_inc(e_sb, 1)
                for u in range(HALF + 1):
                    if u >= 1:
                        root(3, g, u - 1, EPS_LN)
                    if u < HALF:
                        act.wait_ge(n_ps, KC * (HALF * g + u + 1))
                        if u >= 2:
                            act.wait_ge(wo_ps, HALF * g + u - 1)
                        nc.scalar.activation(attT[:, u % 2].rearrange("p k t -> p (k t)"),
                                             ps_o[:, 0:HT], ACT.Copy).then_inc(att_sb, 1)
                    if u >= 1:
                        act.wait_ge(t_norm, HALF * g + u)
                        nc.scalar.activation(rows[:, HALF * g + u - 1], an[:, (u - 1) % 2], ACT.Copy).then_inc(rows_rdy, 1)
                        act.wait_ge(tT_ps, HALF * g + u)
                        if u >= 3:
                            act.wait_ge(g_ps, HALF * g + u - 2)
                        nc.scalar.activation(t2T[:, (u - 1) % 2].rearrange("p k t -> p (k t)"),
                                             ps_t[:, 0:HT], ACT.Copy).then_inc(tT_sb, 1)
            act.wait_ge(r_diff, 1)
            nc.scalar.activation(rt[:, 1], rt[:, 0], ACT.Exp).then_inc(r_exp, 1)

            with act.Fori(0, E // 2) as i:
                for q in range(2):
                    for j in range(WP):
                        act.wait_ge(hm_ps, WP * (2 * i + q) + j + 1)
                        nc.scalar.activation(
                            hmT[:, q, 4 * j:4 * j + 4].rearrange("p (b k) t -> p b (k t)", b=2),
                            ps_h[j % 2][:, :, 0:2 * CAP], ACT.Gelu).then_inc(g_sb, 1)

        @block.vector
        def _(dve):
            STEPS = 72

            def front(g):
                st = Steps(dve, STEPS * g)

                def moments(r, u, src, eps):
                    n = src.shape[-1] // C
                    for b in range(n):
                        ins = nc.vector.bn_stats(stats[:, r, b], src[:, b * C:(b + 1) * C])
                        if b == n - 1:
                            st.done(ins, alone=True)
                    st.done(nc.vector.bn_aggr(mv[:, r, u], stats[:, r, 0:n].rearrange("p a b -> p (a b)")))
                    nc.vector.tensor_scalar(mv[:, r, u, 1:2], mv[:, r, u, 1:2], eps, None, ALU.add).then_inc(mv_rdy, 1)

                def normed(r, u, dst, src):
                    dve.wait_ge(std_rdy, 4 * HALF * g + order.index((r, u)) + 1)
                    st.done(nc.vector.reciprocal(rstd[:, r, u:u + 1], std[:, r, u:u + 1]))
                    return nc.vector.tensor_scalar(dst, src, mv[:, r, u, 0:1], rstd[:, r, u:u + 1],
                                                   ALU.subtract, ALU.mult)

                for s in range(HALF + 2):
                    if s < HALF:
                        apart(dve, x_in[s % 2], 32 * g + 16 * (s // 2 + 1))
                        moments(0, s, xt[:, s % 2], EPS_TOK)
                        normed(0, s, xt[:, s % 2], xt[:, s % 2]).then_inc(x_norm, 1)
                    if 0 <= s - 1 < HALF:
                        u = s - 1
                        hn = h2[:, HALF * g + u]
                        dve.wait_ge(h_ps, HALF * g + u + 1)
                        st.done(nc.vector.tensor_tensor(hn, ps_p[0:TT, u % 2], bcst[:, 2], ALU.add),
                                alone=True)
                        moments(1, u, hn, EPS_TOK)
                        normed(1, u, hn, hn).then_inc(h_norm, 1)
                    if 0 <= s - 2 < HALF:
                        u = s - 2
                        apart(dve, h_rdy, HALF * g + u + 1)
                        moments(2, u, h2[:, HALF * g + u], EPS_LN)
                        if u >= 2:
                            dve.wait_ge(aT_ps, HALF * g + u - 1)
                        normed(2, u, an[:, u % 2], h2[:, HALF * g + u]).then_inc(a_norm, 1)
                for j in range(2 * KC):
                    dve.wait_ge(e_sb, 2 * KC * g + j + 1)
                    st.done(nc.vector.tensor_scalar(ebuf[:, j % 2], ebuf[:, j % 2], 1.0, None, ALU.min))
                    dst = (kT if j % 2 == 0 else qT)[:, j // 2]
                    nc.vector.scalar_tensor_tensor(dst, ps_p[:, j % 2, 0:HT], 0.0, ebuf[:, j % 2],
                                                   ALU.max, ALU.add).then_inc(qk_sb, 1)

                def weighted(m):
                    k3 = kT[:, m].rearrange("p (b s) -> p b s", s=NPATCH)
                    q3 = qT[:, m].rearrange("p (b s) -> p b s", s=NPATCH)
                    e3 = ebuf[:, m % 2].rearrange("p (b s) -> p b s", s=NPATCH)
                    st.done(nc.vector.reduce_sum(ksum[:, m], k3, AX_X))
                    nc.vector.tensor_tensor(e3, q3, ksum[:, m].unsqueeze(2).to_broadcast(q3.shape),
                                            ALU.mult).then_inc(qks_rdy, 1)

                def scaled(m):
                    dve.wait_ge(den_ps, KC * g + m + 1)
                    st.done(nc.vector.tensor_scalar(ebuf[:, m % 2], ps_p[:, m % 2, 0:HT], EPS_Z, None, ALU.add))
                    st.done(nc.vector.reciprocal(ebuf[:, m % 2], ebuf[:, m % 2]))
                    nc.vector.tensor_tensor(qT[:, m], qT[:, m], ebuf[:, m % 2], ALU.mult).then_inc(qn_rdy, 1)

                dve.wait_ge(qk_sb, 2 * KC * (g + 1))
                weighted(0)
                for m in range(KC):
                    if m + 1 < KC:
                        if m >= 1:
                            dve.wait_ge(qn_rdy, KC * g + m)
                        weighted(m + 1)
                    scaled(m)

                def residual(u):
                    t = HALF * g + u
                    dve.wait_ge(wo_ps, t + 1)
                    nc.vector.tensor_tensor(h2[:, t], h2[:, t], ps_p[0:TT, 0], ALU.add).then_inc(h2_rdy, 1)
                    apart(dve, h2_rdy, t + 1)
                    moments(3, u, h2[:, t], EPS_LN)
                    if u >= 2:
                        dve.wait_ge(tT_sb, t - 1)
                    normed(3, u, an[:, u % 2], h2[:, t]).then_inc(t_norm, 1)

                def keep_logits(u):
                    t = HALF * g + u
                    dve.wait_ge(g_ps, t + 1)
                    nc.vector.tensor_copy(logits[:, t], ps_p[0:TT, 1, 0:E]).then_inc(lg_sb, 1)

                for n in range(HALF * KC):
                    u, m = n // KC, n % KC
                    dve.wait_ge(s_ps, HALF * KC * g + n + 1)
                    if n >= 2:
                        dve.wait_ge(n_ps, HALF * KC * g + n - 1)
                    mask = cst[0:TT, CO_MASK:CO_MASK + TT].unsqueeze(1).to_broadcast([TT, HPB, TT])
                    nc.vector.tensor_tensor(ssb[:, n % 2].rearrange("p (h t) -> p h t", h=HPB),
                                            ps_s[0:TT, n % 2, 0:HPB * TT].rearrange("p (h t) -> p h t", h=HPB),
                                            mask, ALU.mult).then_inc(s_sb, 1)
                    if m == 2 and u >= 2:
                        keep_logits(u - 2)
                    if m == 2 and u >= 1:
                        residual(u - 1)
                keep_logits(HALF - 2)
                residual(HALF - 1)
                keep_logits(HALF - 1)
                dve.wait_ge(lg_sb, HALF * (g + 1))
                assert st.n == STEPS, st.n

            dve.wait_ge(bias_ps, 1)
            dve.wait_ge(c_in, 16)
            dve.wait_ge(v_in, 48)
            nc.vector.tensor_tensor(bcst[:, 2], bcst[:, 2], ps_p[0:TT, 0], ALU.add).then_inc(bias_sb, 1)
            dve.wait_ge(bias_sb, 1)
            with dve.Fori(0, 2) as g:
                front(g)

            st = Steps(dve, 2 * STEPS)
            dve.wait_ge(lg_sb, NT)
            nc.vector.memset(hmT[:, 0, 0:KI // 2], 0.0).then_inc(z_set, 1)
            nc.vector.memset(eT[:], 0.0).then_inc(eT_rdy, 1)
            nc.vector.tensor_copy(trib[:], cst[0:TT, CO_TRI:CO_TRI + 2 * TT])
            t3 = lambda n: rt[:, n].rearrange("p (t e) -> p t e", e=E)
            per = lambda a: a.unsqueeze(2).to_broadcast([TT, NT, E])
            st.done(nc.vector.reduce_max(rs[:, 0], logits[:], AX_X))
            nc.vector.tensor_tensor(t3(0), logits[:], per(rs[:, 0]), ALU.subtract).then_inc(r_diff, 1)
            st.done(nc.vector.tensor_tensor(t3(2), logits[:], per(rs[:, 0]), ALU.is_equal))
            st.done(nc.vector.tensor_tensor(rt[:, 3], rt[:, 2], cst[0:TT, CO_REV:CO_REV + NT * E], ALU.mult))
            st.done(nc.vector.reduce_max(rs[:, 1], t3(3), AX_X))
            st.done(nc.vector.tensor_tensor(t3(4), t3(3), per(rs[:, 1]), ALU.is_equal))
            nc.vector.tensor_copy(ohb[:], rt[:, 4]).then_inc(r_oh, 1)
            st.done(nc.vector.tensor_tensor(rt[:, 5], rt[:, 4], cst[0:TT, CO_OFF:CO_OFF + NT * E], ALU.mult))
            st.done(nc.vector.reduce_sum(rs[:, 2], t3(5), AX_X))
            dve.wait_ge(r_exp, 1)
            st.done(nc.vector.reduce_sum(rs[:, 3], t3(1), AX_X))
            st.done(nc.vector.reciprocal(rs[:, 4], rs[:, 3]))
            dve.wait_ge(r_ps, 1)
            st.done(nc.vector.tensor_tensor(rt[:, 6], rt[:, 4], ps_p[0:TT, 0, 0:NT * E], ALU.mult))
            st.done(nc.vector.reduce_sum(rs[:, 5], t3(6), AX_X))
            st.done(nc.vector.tensor_scalar(rs[:, 6], rs[:, 5], float(CAP), None, ALU.is_lt))
            nc.vector.tensor_tensor(prob[:], rs[:, 4], rs[:, 6], ALU.mult)
            st.done(nc.vector.tensor_tensor(rs[:, 7], rs[:, 5], rs[:, 2], ALU.add))
            st.done(nc.vector.tensor_tensor(rs[:, 0], rs[:, 7], cst[0:TT, CO_TOK:CO_TOK + NT], ALU.subtract))
            st.done(nc.vector.tensor_tensor(rs[:, 1], rs[:, 0], rs[:, 6], ALU.mult))
            st.done(nc.vector.tensor_tensor(rs[:, 2], rs[:, 1], cst[0:TT, CO_TOK:CO_TOK + NT], ALU.add))
            st.done(nc.vector.tensor_copy(dst_idx[:], rs[:, 2]))
            st.done(nc.vector.tensor_scalar(rs[:, 3], rs[:, 7], float(CAP), None, ALU.add))
            st.done(nc.vector.tensor_tensor(rs[:, 4], rs[:, 3], rs[:, 6], ALU.mult))
            nc.vector.tensor_copy(src_idx[:], rs[:, 4]).then_inc(idx_rdy, 1)

            dve.wait_ge(rowT_ps, 1)
            nc.vector.tensor_copy(xTe[:, 0].rearrange("p (b k) t -> p b (k t)", b=2),
                                  ps_s[:, :, 0:2 * CAP]).then_inc(rowT_sb, 1)
            with dve.Fori(0, E // 2) as i:
                for q in range(2):
                    e = 2 * i + q
                    dve.wait_ge(oT_ps, e + 1)
                    dve.wait_ge(eo_free, e + 1)
                    nc.vector.tensor_copy(eorow[:, 1 - q], ps_s[0:CH, :, :]).then_inc(eo_rdy, 1)
                    dve.wait_ge(rowT_ps, e + 2)
                    nc.vector.tensor_copy(xTe[:, 1 - q].rearrange("p (b k) t -> p b (k t)", b=2),
                                          ps_s[:, :, 0:2 * CAP]).then_inc(rowT_sb, 1)
                    dve.wait_ge(ew_ps, WP * (e + 1))
                    for b in range(2):
                        ins = nc.vector.tensor_copy(eT[:, q, 2 * b:2 * b + 2].rearrange("p k t -> p (k t)"),
                                                    ps_e[b][:, 0:2 * CAP])
                    ins.then_inc(eT_rdy, 1)
            dve.wait_ge(oT_ps, E + 1)
            dve.wait_ge(eo_free, E + 1)
            nc.vector.tensor_copy(eorow[:, (E - 1) % 2], ps_s[0:CH, :, :]).then_inc(eo_rdy, 1)
            dve.wait_ge(gath, 16 * NT)
            for t in range(NT):
                nc.vector.scalar_tensor_tensor(h2[:, t], rows[:, t], prob[:, t:t + 1], h2[:, t],
                                               ALU.mult, ALU.add).then_inc(o_rdy, 1)

        @block.tensor
        def _(pe):
            def mm(o, a, b, first, last, **kw):
                return nc.tensor.matmul(o, a, b, start=first, stop=last, **kw)

            pe.wait_ge(wtok_in, 16)
            pe.wait_ge(v_in, 48)
            for k in range(KX):
                ins = mm(ps_p[0:TT, 0], vec[:, KX + k:KX + k + 1].to_broadcast([P, TT]), wtok[:, k], k == 0, k == KX - 1)
            ins.then_inc(bias_ps, 1)
            pe.wait_ge(c_in, 16)
            pe.wait_ge(bias_sb, 1)

            def front(g):
                for s in range(HALF + 3):
                    if s < HALF:
                        pe.wait_ge(x_norm, HALF * g + s + 1)
                        if s >= 1:
                            pe.wait_ge(xT_sb, HALF * g + s)
                        for k in range(KX):
                            ins = nc.tensor.transpose(ps_x[:, k // 4, (k % 4) * TT:(k % 4 + 1) * TT],
                                                      xt[:, s % 2, k * P:(k + 1) * P], ident[0:TT, 0:TT])
                        ins.then_inc(xT_ps, 1)
                    if 0 <= s - 3 < HALF:
                        u = s - 3
                        pe.wait_ge(a_norm, HALF * g + u + 1)
                        if u >= 1:
                            pe.wait_ge(aT_sb, HALF * g + u)
                        for k in range(KC):
                            ins = nc.tensor.transpose(ps_t[:, k * TT:(k + 1) * TT],
                                                      an[:, u % 2, k * P:(k + 1) * P], ident[0:TT, 0:TT])
                        ins.then_inc(aT_ps, 1)
                    if 0 <= s - 1 < HALF:
                        u = s - 1
                        pe.wait_ge(xT_sb, HALF * g + u + 1)
                        if u == 0:
                            pe.wait_ge(w_scaled, KX)
                        if u >= 2:
                            pe.wait_ge(h_norm, HALF * g + u - 1)
                        for k in range(KX):
                            ins = mm(ps_p[0:TT, u % 2], xT[:, u % 2, k], wtok[:, k], k == 0, k == KX - 1)
                        ins.then_inc(h_ps, 1)
                pe.wait_ge(wv_in, 16)
                for u in range(HALF):
                    pe.wait_ge(aT_sb, HALF * g + u + 1)
                    if u < 2:
                        pe.wait_ge(h_norm, HALF * g + u + 3)
                    else:
                        pe.wait_ge(v_sb, HALF * g + u - 1)
                    for k in range(KC):
                        ins = mm(ps_p[0:TT, u % 2], anT[:, k, u * TT:(u + 1) * TT], wvs[:, k], k == 0, k == KC - 1)
                    ins.then_inc(v_ps, 1)
                pe.wait_ge(wk_in, 16)
                pe.wait_ge(wq_in, 16)
                for j in range(2 * KC):
                    w, m = (wks, wqs)[j % 2], j // 2
                    if j < 2:
                        pe.wait_ge(v_sb, HALF * g + j + 3)
                    else:
                        pe.wait_ge(qk_sb, 2 * KC * g + j - 1)
                    for k in range(KC):
                        ins = mm(ps_p[:, j % 2, 0:HT], w[:, k, m * P:(m + 1) * P], anT[:, k], k == 0, k == KC - 1)
                    ins.then_inc(qk_ps, 1)
                for m in range(KC):
                    pe.wait_ge(qks_rdy, KC * g + m + 1)
                    if m >= 2:
                        pe.wait_ge(qn_rdy, KC * g + m - 1)
                    mm(ps_p[:, m % 2, 0:HT], cst[:, CO_BLK:CO_BLK + P], ebuf[:, m % 2], True, True).then_inc(den_ps, 1)

                def scores(n):
                    u, m = n // KC, n % KC
                    pe.wait_ge(qb_rdy, HALF * KC * g + n + 1)
                    if n >= 2:
                        pe.wait_ge(s_sb, HALF * KC * g + n - 1)
                    mm(ps_s[0:TT, n % 2, 0:HPB * TT], kT[:, m, u * TT:(u + 1) * TT], qblk[:, n % 2],
                       True, True).then_inc(s_ps, 1)

                def numerators(n):
                    u, m = n // KC, n % KC
                    pe.wait_ge(s_sb, HALF * KC * g + n + 1)
                    if m == 0 and u >= 1:
                        pe.wait_ge(att_sb, HALF * g + u)
                    for h in range(HPB):
                        ins = mm(ps_o[DH * h:DH * (h + 1), m * TT:(m + 1) * TT],
                                 vsb[:, u, m * P + DH * h:m * P + DH * (h + 1)],
                                 ssb[:, n % 2, h * TT:(h + 1) * TT], True, True)
                    ins.then_inc(n_ps, 1)

                def projected(u):
                    t = HALF * g + u
                    pe.wait_ge(att_sb, t + 1)
                    if u == 0:
                        pe.wait_ge(wo_in, 16)
                        pe.wait_ge(qn_rdy, KC * (g + 1))
                    else:
                        pe.wait_ge(h2_rdy, t)
                    for k in range(KC):
                        ins = mm(ps_p[0:TT, 0], attT[:, u % 2, k], wos[:, k], k == 0, k == KC - 1)
                    ins.then_inc(wo_ps, 1)

                def rows_turned(u):
                    t = HALF * g + u
                    pe.wait_ge(t_norm, t + 1)
                    if u >= 1:
                        pe.wait_ge(tT_sb, t)
                    for k in range(KC):
                        ins = nc.tensor.transpose(ps_t[:, k * TT:(k + 1) * TT], an[:, u % 2, k * P:(k + 1) * P],
                                                  ident[0:TT, 0:TT])
                    ins.then_inc(tT_ps, 1)

                def gated(u):
                    t = HALF * g + u
                    pe.wait_ge(tT_sb, t + 1)
                    if u >= 1:
                        pe.wait_ge(lg_sb, t)
                    for k in range(KC):
                        ins = mm(ps_p[0:TT, 1, 0:E], t2T[:, u % 2, k], gsb[:, k], k == 0, k == KC - 1)
                    ins.then_inc(g_ps, 1)

                scores(0)
                for n in range(HALF * KC):
                    u, m = n // KC, n % KC
                    if n + 1 < HALF * KC:
                        scores(n + 1)
                    numerators(n)
                    if m == 1 and u >= 2:
                        gated(u - 2)
                    if m == 1 and u >= 1:
                        projected(u - 1)
                    if m == 3 and u >= 1:
                        rows_turned(u - 1)
                gated(HALF - 2)
                projected(HALF - 1)
                rows_turned(HALF - 1)
                gated(HALF - 1)
                pe.wait_ge(lg_sb, HALF * (g + 1))

            with pe.Fori(0, 2) as g:
                front(g)

            pe.wait_ge(r_oh, 1)
            for d in range(NT):
                ins = mm(ps_p[0:TT, 0, E * d:E * NT], trib[:, TT * min(d, 1):TT * (min(d, 1) + 1)],
                         ohb[:, 0:E * (NT - d)], d == 0, d == NT - 1, skip_group_check=True)
            ins.then_inc(r_ps, 1)

            def slots_turned(e, q):
                pe.wait_ge(xrow_in[q], 8 * (e - q) + 16)
                for k in range(KC):
                    for c in range(2):
                        ins = nc.tensor.transpose(
                            ps_s[:, k // 2, (k % 2) * CAP + c * CH:(k % 2) * CAP + (c + 1) * CH],
                            xrow[:, q, c, k * P:(k + 1) * P], ident[0:CH, 0:CH])
                ins.then_inc(rowT_ps, 1)

            def outputs_turned(e, q):
                for c in range(2):
                    for m in range(KC):
                        ins = nc.tensor.transpose(ps_s[0:CH, c, m * P:(m + 1) * P],
                                                  eT[:, q, m, c * CH:(c + 1) * CH], ident)
                ins.then_inc(oT_ps, 1)

            slots_turned(0, 0)
            pe.wait_ge(idx_rdy, 1)
            with pe.Fori(0, E // 2) as i:
                for q in range(2):
                    e = 2 * i + q
                    for j in range(WP):
                        s = q * PIECES + j
                        pe.wait_ge(slot_in[s], 16 * i + 16)
                        if j == 0:
                            pe.wait_ge(rowT_sb, e + 1)
                        if j >= 2:
                            pe.wait_ge(g_sb, WP * e + j - 1)
                        for c in range(4):
                            for k in range(KC):
                                ins = mm(ps_h[j % 2][:, c // 2, (c % 2) * CAP:(c % 2 + 1) * CAP],
                                         ring[s][:, k, c * P:(c + 1) * P], xTe[:, q, k], k == 0, k == KC - 1)
                        ins.then_inc(hm_ps, 1)
                        if j == 1:
                            pe.wait_ge(eT_rdy, e + 1)
                            outputs_turned(e - 1, 1 - q)
                        if j == 3:
                            pe.wait_ge(eo_rdy, e + 1)
                            slots_turned(e + 1, 1 - q)
                    for j in range(WP):
                        s = q * PIECES + WP + j
                        pe.wait_ge(slot_in[s], 16 * i + 16)
                        pe.wait_ge(g_sb, WP * e + j + 1)
                        for b in range(4):
                            for m in range(KC):
                                ins = mm(ps_e[m // 2][:, (m % 2) * CAP:(m % 2 + 1) * CAP],
                                         ring[s][:, b, m * P:(m + 1) * P], hmT[:, q, 4 * j + b],
                                         j == 0 and b == 0 and m % 2 == 0, j == WP - 1 and b == 3,
                                         skip_group_check=True)
                        ins.then_inc(ew_ps, 1)
                    pe.wait_ge(rowT_sb, e + 2)
            pe.wait_ge(eT_rdy, E + 1)
            outputs_turned(E - 1, (E - 1) % 2)


def kernel(x, L0_tok_W, L0_tok_b, L0_tok_g1, L0_tok_b1, L0_tok_g2, L0_tok_b2, L0_attn_cos, L0_attn_sin,
           L0_attn_Wq, L0_attn_Wk, L0_attn_Wv, L0_attn_Wo, L0_ffn_gate_weight, L0_ffn_wi, L0_ffn_wo):
    import concourse.bacc as bacc
    from concourse.bass_utils import run_bass_kernel_spmd

    a = np.asarray
    t = lambda w: np.ascontiguousarray(a(w).T)
    by_partition = lambda v: a(v).reshape(KX, P).T
    ins = {
        "x": np.ascontiguousarray(a(x)[:, :NPATCH * TIN]).reshape(TOKENS, IN_DIM),
        "w_tok": a(L0_tok_W),
        "cols": np.ascontiguousarray(np.concatenate([by_partition(L0_tok_g1), by_partition(L0_tok_b1)], 1)),
        "g2b2b": np.stack([a(L0_tok_g2), a(L0_tok_b2), a(L0_tok_b)]),
        "wq": t(L0_attn_Wq), "wk": t(L0_attn_Wk), "wv": t(L0_attn_Wv), "wo": t(L0_attn_Wo),
        "gate": t(L0_ffn_gate_weight),
        "wi": a(L0_ffn_wi), "wout": a(L0_ffn_wo),
        "consts": constants(),
    }
    nc = bacc.Bacc("TRN2", target_bir_lowering=False, num_devices=1)
    args = {n: nc.dram_tensor(f"in_{n}", v.shape, F32, kind="ExternalInput").ap() for n, v in ins.items()}
    args["out"] = nc.dram_tensor("out_0", (TOKENS, C), F32, kind="ExternalOutput").ap()
    audio_tower(nc, **args)
    r = run_bass_kernel_spmd(nc, [{f"in_{n}": v for n, v in ins.items()}], core_ids=[0])
    return r.results[0]["out_0"].reshape(BATCH, NPATCH, C)
```

```python
from contextlib import ExitStack

import numpy as np
import concourse.bass as bass
from concourse import mybir

F32 = mybir.dt.float32
F32R = mybir.dt.float32r
BF16 = mybir.dt.bfloat16
U32 = mybir.dt.uint32
ALU = mybir.AluOpType
ACT = mybir.ActivationFunctionType
AX_X = mybir.AxisListType.X

P = 128
BATCH, SEQ, FEAT = 64, 250, 64
TIN = 16
NPATCH = SEQ // TIN
IN_DIM = TIN * FEAT
C = 512
TOKENS = BATCH * NPATCH
BT = 8
TT = BT * NPATCH
NT = TOKENS // TT
HALF = NT // 2
HT = HALF * TT
KX = IN_DIM // P
KC = C // P
DH = 32
HPB = P // DH
E = 8
INTER = 2048
KI = INTER // P
CAP = TOKENS * 5 // 4 // E
CH = CAP // 2
EPS_TOK, EPS_LN, EPS_Z = 1e-6, 1e-5, 1e-6

PIECES = 8
WP = PIECES // 2
SLOTS = 2 * PIECES

XS_ROWS = (E + 2) * CAP
EO_ROWS = (E + 1) * CAP

EMBED_AT = (-25.1, -18.7, -4.5, 3.9, 42.8, 57.4, 71.0, 83.1)
EMBED = {
    "x_stats": (-26.8, -26.8), "x_root": (-17.0, -17.0), "x_norm": (-16.5, -16.5), "x_turn": (-5.1, -5.1),
    "embed": (3.1, 3.1), "h_stats": (1.4, 1.4), "h_root": (8.2, 8.2), "h_norm": (9.2, 9.2),
    "h_affine": (15.4, 15.4), "a_stats": (16.9, 15.8), "a_root": (20.1, 24.7), "a_norm": (19.7, 23.9),
    "a_turn": (26.6, 37.0), "aT_hi": (22.5, 36.4), "aT_lo": (24.9, 40.8), "v": (38.7, 55.7), "v_copy": (38.3, 58.2),
}
XT_EACH = 1.1
XT = {"xT_hi": -8.1, "xT_lo": -8.7,}
QK_AT = ((46.6, 57.2, 63.1, 71.6),
         (131.3, 145.6, 161.1, 179.1))
QK_EACH = 2.5
QK = {"qk": 1.7, "qk_exp": -1.0, "qk_elu": -0.7,}
DEN = {"q_times_sum": 4.5, "den": 15.3, "den_copy": 13.2, "den_inv": 12.8, "q_div": 18.2,}
ATTEND_AT = (91.6, 112.2, 143.5, 163.5, 196.5, 249.8, 278.0, 310.7)
BLOCK_EACH = 5.33
BLOCK = {"q_blocks": -14.5, "scores": -5.9, "mask": -8.8, "attend": 3.1,}
ATTENDED = {
    "att_hi": -5.7, "att_lo": -4.8, "project": 8.1, "residual": 4.3, "t_root": 11.1, "t_norm": 24.4, "t_turn": 40.1,
    "tT_copy": 35.4, "gate": 46.0, "gate_copy": 41.6,
}
WEIGHTS_AT = (-215.3, -99.2, -38.2, 25.2, 31.1, 35.2)
BIAS_AT, BIAS_ADD_AT = -48.3, -41.5


def front_schedule():
    order = []
    for t in range(NT):
        order += [(EMBED_AT[t] + lag[t // HALF], step, t) for step, lag in EMBED.items()]
        for b in range(2):
            order += [(EMBED_AT[t] + XT_EACH * b + lag, step, 2 * t + b) for step, lag in XT.items()]
        for m in range(KC):
            order += [(ATTEND_AT[t] + BLOCK_EACH * m + lag, step, KC * t + m) for step, lag in BLOCK.items()]
        order += [(ATTEND_AT[t] + BLOCK_EACH * KC + lag, step, t) for step, lag in ATTENDED.items()]
    for b in range(2 * KC):
        at = QK_AT[b // KC][b % KC]
        for j in range(2):
            order += [(at + QK_EACH * j + lag, step, 2 * b + j) for step, lag in QK.items()]
        order += [(at + lag, step, b) for step, lag in DEN.items()]
    for n in range(6):
        order += [(WEIGHTS_AT[n], "w_hi", n), (WEIGHTS_AT[n] + 0.1, "w_lo", n)]
    order += [(BIAS_AT, "bias", 0), (BIAS_ADD_AT, "bias_add", 0)]
    order = [(step, i) for _, step, i in sorted(order)]
    for kind in {step for step, _ in order}:
        turns = [i for step, i in order if step == kind]
        assert turns == sorted(turns), kind
    return order


CO_ID = 0
CO_BLK = CO_ID + P
CO_MASK = CO_BLK + P
CO_TRI = CO_MASK + TT
CO_ONE = CO_TRI + TT
CO_HM = CO_ONE + TT
CO_REV = CO_HM + HPB
CO_OFF = CO_REV + NT * E
CO_TOK = CO_OFF + NT * E
CO_N = CO_TOK + NT


def constants():
    c = np.zeros((P, CO_N), np.float32)
    r = np.arange(P)
    c[:, CO_ID:CO_ID + P] = np.eye(P)
    c[:, CO_BLK:CO_BLK + P] = r[:, None] // DH == r[None] // DH
    s = np.arange(TT)
    c[:TT, CO_MASK:CO_MASK + TT] = s[:, None] // NPATCH == s[None] // NPATCH
    c[:TT, CO_TRI:CO_TRI + TT] = s[:, None] < s[None]
    c[:TT, CO_ONE:CO_ONE + TT] = 1
    c[:, CO_HM:CO_HM + HPB] = r[:, None] // DH == np.arange(HPB)[None]
    c[:, CO_REV:CO_REV + NT * E] = np.tile(E - np.arange(E), NT)
    c[:, CO_OFF:CO_OFF + NT * E] = np.tile(CAP * np.arange(E), NT)
    c[:TT, CO_TOK:CO_TOK + NT] = XS_ROWS + s[:, None] + TT * np.arange(NT)[None]
    return c


def audio_tower(nc, x, w_tok, cols, g2b2b, wq, wk, wv, wo, gate, wi, wout, consts, out):
    xs_dram = nc.dram_tensor("xs_rows", (XS_ROWS + TOKENS, C), F32).ap()
    eo_dram = nc.dram_tensor("eo_rows", (EO_ROWS, C), F32).ap()

    with ExitStack() as ctx:
        def psum(name, shape):
            return ctx.enter_context(nc.psum_tensor(name, shape, F32))

        def sem(name):
            return ctx.enter_context(nc.semaphore(name))

        start = (nc.sbuf_base + 63) // 64 * 64
        size = (nc.sbuf_bytes_remaining - 128) // 64 * 64
        ctx.enter_context(nc.sbuf_tensor("arena", [P, size], mybir.dt.uint8))
        at = [start]

        def place(name, shape, dt=F32):
            n = int(np.prod(shape[1:])) * (2 if dt == BF16 else 4)
            t = nc.alloc_sbuf_tensor_at(name, shape, dt, offset=at[0])
            at[0] += (n + 31) // 32 * 32
            assert at[0] <= start + size, (name, at[0] - start - size)
            return t

        def halves(name, shape):
            return place(name + "_hi", shape, F32R), place(name + "_lo", shape, F32R)

        cst = place("cst", [P, CO_N])
        h2 = place("h2", [TT, NT, C])
        logits = place("logits", [TT, NT, E])
        prob = place("prob", [TT, NT])
        src_idx = place("src_idx", [TT, NT], U32)
        mv = place("mv", [TT, 4, NT, 2])
        rstd = place("rstd", [TT, 4, NT])
        shared = at[0]

        wvs = halves("wv", [P, KC, C])
        wks, wqs = halves("wk", [P, KC, C]), halves("wq", [P, KC, C])
        wtok_at = at[0]
        wtok = halves("wtok", [P, KX, C])
        end, at[0] = at[0], wtok_at + 4 * KX * C
        kT1, qT1 = place("kT1", [P, KC, HT]), place("qT1", [P, KC, HT])
        assert at[0] <= end
        at[0] = end
        wos = halves("wo", [P, KC, C])
        bcst = place("bcst", [TT, 3, C])
        vec = place("vec", [P, 2 * KX])
        gsb = place("gsb", [P, KC, E])
        stats = place("stats", [TT, 4, 2, 6])
        std = place("std", [TT, 4, NT])
        ksum = place("ksum", [P, KC, HT // NPATCH])
        xt = place("xt", [TT, 2, IN_DIM])
        xT = halves("xT", [P, KX, TT])
        anT = halves("anT", [P, KC, HT])
        an = place("an", [TT, C])
        tn = place("tn", [TT, C])
        stage_at = at[0]
        kTs, qTs = [place("kT0", [P, KC, HT]), kT1], [place("qT0", [P, KC, HT]), qT1]
        kq = place("kq", [P, HT])
        dsb = place("dsb", [P, HT])
        ebuf = place("ebuf", [P, HT])
        qblk = place("qblk", [P, 2, HPB * TT])
        ssb = place("ssb", [TT, 2, HPB * TT])
        attT = halves("attT", [P, KC, TT])
        t2T = place("t2T", [P, KC, TT])
        vsb = place("vsb", [TT, NT, C])
        end, at[0] = at[0], stage_at
        raw = [place(f"raw{s}", [P, KC, C]) for s in range(3)]
        assert at[0] <= end - 4 * NT * C, "the staging reaches into vsb"

        at[0] = shared
        ring = [place(f"ring{s}", [P, KC, C]) for s in range(SLOTS)]
        xrow = place("xrow", [CH, 2, 2, C])
        xTe = place("xTe", [P, 2, KC, CAP])
        eT = place("eT", [P, 2, KC, CAP])
        eorow = place("eorow", [CH, 2, 2, C])
        hmT = place("hmT", [P, 2, KI, CAP])
        at[0] -= 4 * KI * CAP
        rt = place("rt", [TT, 8, NT * E])
        rs = place("rs", [TT, 8, NT])
        ohb = place("ohb", [TT, NT * E], BF16)
        trib = place("trib", [TT, 2 * TT], BF16)
        dst_idx = place("dst_idx", [TT, NT], U32)
        at[0] = shared + 4 * KC * C * (SLOTS - 2)
        rows = place("rows", [TT, NT, C])

        ident = cst[:, CO_ID:CO_ID + P]

        ps_x = psum("ps_x", [P, 2, 512])
        ps_p = psum("ps_p", [P, 2, 512])
        ps_t = psum("ps_t", [P, 512])
        ps_o = psum("ps_o", [P, 512])
        ps_s = psum("ps_s", [P, 2, 512])
        ps_h = [ps_x, ps_p]
        ps_e = [ps_t, ps_o]

        c_in, vec_in, bcst_in, gate_in = sem("c_in"), sem("vec_in"), sem("bcst_in"), sem("gate_in")
        z_out, z_set = sem("z_out"), sem("z_set")
        w_in = [sem(f"w_in{n}") for n in range(6)]
        x_in = [sem(f"x_in{u}") for u in range(2)]
        slot_in = [sem(f"slot_in{s}") for s in range(SLOTS)]
        scat, eo_out, y_out = sem("scat"), sem("eo_out"), sem("y_out")
        xrow_in = [sem("xrow_in0"), sem("xrow_in1")]
        gath = [sem(f"gath{t}") for t in range(NT)]
        bias_ps, bias_sb, w_hi, w_lo = sem("bias_ps"), sem("bias_sb"), sem("w_hi"), sem("w_lo")
        wt_lo, h_mid = sem("wt_lo"), sem("h_mid")
        mv_rdy, std_rdy = [sem(f"mv_rdy{r}") for r in range(4)], [sem(f"std_rdy{r}") for r in range(4)]
        x_norm, xT_ps, xT_hi, xT_lo, h_ps, h_evac, h_norm, h_mul, h_rdy = (sem(n) for n in (
            "x_norm", "xT_ps", "xT_hi", "xT_lo", "h_ps", "h_evac", "h_norm", "h_mul", "h_rdy"))
        a_norm, aT_ps, aT_hi, aT_lo, v_ps, v_sb, qk_ps, e_sb, qk_sb = (sem(n) for n in (
            "a_norm", "aT_ps", "aT_hi", "aT_lo", "v_ps", "v_sb", "qk_ps", "e_sb", "qk_sb"))
        kq_rdy, den_ps, den_sb, den_inv, qn_rdy, qb_rdy, s_ps, s_sb, n_ps, att_hi, att_lo = (sem(n) for n in (
            "kq_rdy", "den_ps", "den_sb", "den_inv", "qn_rdy", "qb_rdy", "s_ps", "s_sb", "n_ps", "att_hi", "att_lo"))
        wo_ps, h2_rdy, t_norm, tT_ps, tT_sb, g_ps, lg_sb = (sem(n) for n in (
            "wo_ps", "h2_rdy", "t_norm", "tT_ps", "tT_sb", "g_ps", "lg_sb"))
        dve_step = sem("dve_step")
        r_diff, r_exp, r_oh, r_ps, idx_rdy = sem("r_diff"), sem("r_exp"), sem("r_oh"), sem("r_ps"), sem("idx_rdy")
        rows_rdy, eo_free = sem("rows_rdy"), sem("eo_free")
        rowT_ps, rowT_sb, hm_ps, g_sb, ew_ps, eT_rdy, oT_ps, eo_rdy, o_rdy = (sem(n) for n in (
            "rowT_ps", "rowT_sb", "hm_ps", "g_sb", "ew_ps", "eT_rdy", "oT_ps", "eo_rdy", "o_rdy"))

        block = ctx.enter_context(nc.Block())

        x_t = x.rearrange("(t p) d -> t p d", p=TT)
        out_t = out.rearrange("(t p) d -> t p d", p=TT)
        wi_v = wi.rearrange("(i q) (k p) (j n) -> i q j p k n", q=2, p=P, n=C)
        wo_v = wout.rearrange("(i q) (j k p) n -> i q j p k n", q=2, p=P, k=KC)
        xs_v = xs_dram[0:XS_ROWS].rearrange("(i q c p) d -> i q p c d", q=2, c=2, p=CH)
        eo_v = eo_dram.rearrange("(e c p) d -> e p c d", c=2, p=CH)
        by_block = lambda w: w.rearrange("(k p) n -> p k n", p=P)
        weights = [by_block(w_tok)[:, 0:KC], by_block(w_tok)[:, KC:KX], by_block(wv), by_block(wk), by_block(wq), by_block(wo)]
        split_to = [tuple(w[:, 0:KC] for w in wtok), tuple(w[:, KC:KX] for w in wtok), wvs, wks, wqs, wos]

        schedule = front_schedule()
        read_by = {"bias": bias_sb, "embed": h_evac, "v": v_sb, "qk": qk_sb, "den": den_sb, "project": h2_rdy, "gate": lg_sb}
        uses = [step for step in schedule if step[0] in read_by]
        bank = {step: n % 2 for n, step in enumerate(uses)}
        before = {step: (read_by[uses[n - 2][0]], uses[n - 2][1] + 1) if n >= 2 else None for n, step in enumerate(uses)}
        turned = [step for step in schedule if step[0] in ("a_turn", "t_turn")]
        before_t = {step: ((aT_lo if turned[n - 1][0] == "a_turn" else tT_sb), turned[n - 1][1] + 1) if n else None
                    for n, step in enumerate(turned)}

        class Steps:

            def __init__(self, eng):
                self.eng, self.n = eng, 0

            def done(self, ins):
                self.n += 1
                ins.then_inc(dve_step, 1)
                self.eng.wait_ge(dve_step, self.n)

        @block.sync
        def _(sp):
            def load_w(n):
                sp.dma_start(raw[n % 3][:], weights[n]).then_inc(w_in[n], 16)

            sp.dma_start(xt[:, 0], x_t[0]).then_inc(x_in[0], 16)
            sp.dma_start(vec[:], cols).then_inc(vec_in, 16)
            sp.dma_start(cst[:], consts).then_inc(c_in, 16)
            load_w(0)
            load_w(1)
            sp.dma_start(xt[:, 1], x_t[1]).then_inc(x_in[1], 16)
            sp.dma_start(bcst[:], g2b2b.partition_broadcast(TT)).then_inc(bcst_in, 16)
            load_w(2)
            sp.dma_start(gsb[:], gate.rearrange("(k p) e -> p k e", p=P)).then_inc(gate_in, 16)
            for t in range(2, NT):
                sp.wait_ge(xT_ps, t - 1)
                sp.dma_start(xt[:, t % 2], x_t[t]).then_inc(x_in[t % 2], 16)
                if t < 5:
                    n = t + 1
                    if n < 5:
                        sp.wait_ge(wt_lo, n - 2)
                        sp.wait_ge(bias_ps, 1)
                    else:
                        sp.wait_ge(w_lo, 1)
                    load_w(n)
            sp.wait_ge(z_set, 1)
            z = h2[0:CH, NT - 2:NT].rearrange("p c d -> p (c d)")
            for e in range(E + 2):
                sp.dma_start(xs_v[e // 2, e % 2], z.rearrange("p (c d) -> p c d", c=2)).then_inc(z_out, 16)

            def piece(i, s):
                q, j = s // PIECES, s % PIECES
                src = wi_v[i, q, j] if j < WP else wo_v[i, q, j - WP]
                sp.dma_start(ring[s][:], src).then_inc(slot_in[s], 16)

            sp.wait_ge(v_ps, NT)
            for s in range(0, 2):
                piece(0, s)
            sp.wait_ge(qk_ps, 4 * KC)
            for s in range(2, 6):
                piece(0, s)
            sp.wait_ge(h_ps, NT)
            for s in range(6, 8):
                piece(0, s)
            sp.wait_ge(scat, 16 * NT)
            sp.wait_ge(xrow_in[0], 16)
            sp.wait_ge(xrow_in[1], 16)
            for s in range(8, SLOTS):
                piece(0, s)
            with sp.Fori(1, E // 2) as i:
                for s in range(SLOTS):
                    q, j = s // PIECES, s % PIECES
                    used = hm_ps if j < WP else ew_ps
                    sp.wait_ge(used, 2 * WP * i + (q * WP + j % WP + 1 - 2 * WP))
                    piece(i, s)
            for t in range(NT):
                sp.wait_ge(o_rdy, t + 1)
                sp.dma_start(out_t[t], h2[:, t]).then_inc(y_out, 16)
            sp.wait_ge(y_out, 16 * NT)

        @block.gpsimd
        def _(pool):
            nc.gpsimd.memset(h2[:, NT - 2:NT], 0.0).then_inc(z_set, 1)
            pool.wait_ge(c_in, 16)
            pool.wait_ge(bcst_in, 16)
            for step, i in schedule:
                if step == "h_affine":
                    pool.wait_ge(h_norm, i + 1)
                    nc.gpsimd.tensor_tensor(h2[:, i], h2[:, i], bcst[:, 0], ALU.mult).then_inc(h_mul, 1)
                    pool.wait_ge(h_mul, i + 1)
                    nc.gpsimd.tensor_tensor(h2[:, i], h2[:, i], bcst[:, 1], ALU.add).then_inc(h_rdy, 1)
                elif step == "w_lo" and i >= 2:
                    pool.wait_ge(w_hi, i + 1)
                    nc.gpsimd.tensor_tensor(split_to[i][1][:], raw[i % 3][:], split_to[i][0][:].bitcast(F32),
                                            ALU.subtract).then_inc(w_lo, 1)
                elif step == "q_div":
                    pool.wait_ge(den_inv, i + 1)
                    qm = qTs[i // KC][:, i % KC]
                    nc.gpsimd.tensor_tensor(qm, qm, dsb[:], ALU.mult).then_inc(qn_rdy, 1)
                elif step == "q_blocks":
                    g, u, m = i // (HALF * KC), i // KC % HALF, i % KC
                    pool.wait_ge(qn_rdy, KC * g + m + 1)
                    if i >= 2:
                        pool.wait_ge(s_ps, i - 1)
                    q4 = qTs[g][:, m, u * TT:(u + 1) * TT].unsqueeze(1).to_broadcast([P, HPB, TT])
                    hm4 = cst[:, CO_HM:CO_HM + HPB].unsqueeze(2).to_broadcast([P, HPB, TT])
                    nc.gpsimd.tensor_tensor(qblk[:, i % 2].rearrange("p (h t) -> p h t", h=HPB),
                                            q4, hm4, ALU.mult).then_inc(qb_rdy, 1)
            pool.wait_ge(z_out, 16 * (E + 2))
            pool.wait_ge(idx_rdy, 1)
            for t in range(NT):
                pool.wait_ge(rows_rdy, t + 1)
                pool.indirect_dma_start(
                    out=xs_dram, out_offset=bass.IndirectOffsetOnAxis(ap=dst_idx[:, t:t + 1], axis=0),
                    in_=rows[:, t], in_offset=None).then_inc(scat, 16)
            pool.wait_ge(scat, 16 * NT)
            for q in range(2):
                pool.dma_start(xrow[:, q], xs_v[0, q]).then_inc(xrow_in[q], 16)
            pool.sem_inc(eo_free, 2)
            with pool.Fori(0, E // 2) as i:
                for q in range(2):
                    pool.wait_ge(eo_rdy, 2 * i + q + 1)
                    pool.dma_start(eo_v[2 * i + q], eorow[:, 1 - q]).then_inc(eo_out, 16)
                    pool.wait_ge(rowT_ps, 2 * i + q + 1)
                    pool.dma_start(xrow[:, q], xs_v[i + 1, q]).then_inc(xrow_in[q], 16)
                    pool.wait_ge(eo_out, 32 * i + 16 * (q + 1))
                    pool.sem_inc(eo_free, 1)
            pool.wait_ge(eo_rdy, E + 1)
            pool.dma_start(eo_v[E], eorow[:, (E - 1) % 2]).then_inc(eo_out, 16)
            pool.wait_ge(xrow_in[0], 16 * (E // 2 + 1))
            pool.wait_ge(xrow_in[1], 16 * (E // 2 + 1))
            pool.wait_ge(eo_out, 16 * (E + 1))
            for t in range(NT):
                pool.indirect_dma_start(
                    out=rows[:, t], out_offset=None, in_=eo_dram,
                    in_offset=bass.IndirectOffsetOnAxis(ap=src_idx[:, t:t + 1], axis=0)).then_inc(gath[t], 16)
            for t in range(NT):
                pool.wait_ge(gath[t], 16)

        @block.scalar
        def _(act):
            def root(r, t):
                act.wait_ge(mv_rdy[r], t + 1)
                nc.scalar.activation(std[:, r, t:t + 1], mv[:, r, t, 1:2], ACT.Sqrt).then_inc(std_rdy[r], 1)

            for step, i in schedule:
                if step == "w_hi":
                    act.wait_ge(w_in[i], 16)
                    act.wait_ge(vec_in, 16)
                    if i < 2:
                        for k in range(KC):
                            ins = nc.scalar.activation(split_to[i][0][:, k], raw[i][:, k], ACT.Copy,
                                                       scale=vec[:, KC * i + k:KC * i + k + 1])
                    else:
                        ins = nc.scalar.activation(split_to[i][0][:], raw[i % 3][:], ACT.Copy)
                    ins.then_inc(w_hi, 1)
                elif step == "x_root":
                    root(0, i)
                elif step == "h_root":
                    root(1, i)
                elif step == "a_root":
                    root(2, i)
                elif step == "t_root":
                    root(3, i)
                elif step == "xT_hi":
                    t, b = i // 2, i % 2
                    act.wait_ge(xT_ps, t + 1)
                    if t >= 1:
                        act.wait_ge((h_mid, h_ps)[b], t)
                    nc.scalar.activation(xT[0][:, KC * b:KC * (b + 1)].rearrange("p k t -> p (k t)"),
                                         ps_x[:, b, 0:HT], ACT.Copy).then_inc(xT_hi, 1)
                elif step == "aT_hi":
                    u = i % HALF
                    act.wait_ge(aT_ps, i + 1)
                    if i >= HALF:
                        act.wait_ge(qk_ps, 2 * KC)
                        act.wait_ge(v_ps, HALF)
                    nc.scalar.activation(anT[0][:, :, u * TT:(u + 1) * TT],
                                         ps_t[:, 0:HT].rearrange("p (k t) -> p k t", k=KC), ACT.Copy).then_inc(aT_hi, 1)
                elif step == "v_copy":
                    act.wait_ge(v_ps, i + 1)
                    nc.scalar.activation(vsb[:, i], ps_p[0:TT, bank["v", i]], ACT.Copy).then_inc(v_sb, 1)
                elif step == "qk_exp":
                    act.wait_ge(qk_ps, i + 1)
                    if i == 0:
                        act.wait_ge(w_lo, 4)
                    if i >= 1:
                        act.wait_ge(qk_sb, i)
                    nc.scalar.activation(ebuf[:], ps_p[:, bank["qk", i], 0:HT], ACT.Exp).then_inc(e_sb, 1)
                elif step == "den_copy":
                    act.wait_ge(den_ps, i + 1)
                    if i >= 1:
                        act.wait_ge(qn_rdy, i)
                    nc.scalar.activation(dsb[:], ps_p[:, bank["den", i], 0:HT], ACT.Copy, bias=EPS_Z).then_inc(den_sb, 1)
                elif step == "att_hi":
                    act.wait_ge(n_ps, KC * (i + 1))
                    if i >= 1:
                        act.wait_ge(wo_ps, i)
                    nc.scalar.activation(attT[0][:].rearrange("p k t -> p (k t)"),
                                         ps_o[:, 0:HT], ACT.Copy).then_inc(att_hi, 1)
                elif step == "tT_copy":
                    act.wait_ge(tT_ps, i + 1)
                    if i >= 1:
                        act.wait_ge(g_ps, i)
                    nc.scalar.activation(t2T[:].rearrange("p k t -> p (k t)"),
                                         ps_t[:, 0:HT], ACT.Copy).then_inc(tT_sb, 1)
            act.wait_ge(r_diff, 1)
            nc.scalar.activation(rt[:, 1], rt[:, 0], ACT.Exp).then_inc(r_exp, 1)

            with act.Fori(0, E // 2) as i:
                for q in range(2):
                    for j in range(WP):
                        act.wait_ge(hm_ps, WP * (2 * i + q) + j + 1)
                        nc.scalar.activation(
                            hmT[:, q, 4 * j:4 * j + 4].rearrange("p (b k) t -> p b (k t)", b=2),
                            ps_h[j % 2][:, :, 0:2 * CAP], ACT.Gelu).then_inc(g_sb, 1)

        @block.vector
        def _(dve):
            st = Steps(dve)

            def moments(r, t, src, eps):
                n = src.shape[-1] // C
                for b in range(n):
                    ins = nc.vector.bn_stats(stats[:, r, b], src[:, b * C:(b + 1) * C])
                st.done(ins)
                st.done(nc.vector.bn_aggr(mv[:, r, t], stats[:, r, 0:n].rearrange("p a b -> p (a b)")))
                nc.vector.tensor_scalar(mv[:, r, t, 1:2], mv[:, r, t, 1:2], eps, None, ALU.add).then_inc(mv_rdy[r], 1)

            def normed(r, t, dst, src):
                dve.wait_ge(std_rdy[r], t + 1)
                st.done(nc.vector.reciprocal(rstd[:, r, t:t + 1], std[:, r, t:t + 1]))
                return nc.vector.tensor_scalar(dst, src, mv[:, r, t, 0:1], rstd[:, r, t:t + 1],
                                               ALU.subtract, ALU.mult)

            def rest(lo, src, hi):
                return nc.vector.tensor_tensor(lo, src, hi.bitcast(F32), ALU.subtract)

            dve.wait_ge(c_in, 16)
            for step, i in schedule:
                if step == "w_lo" and i < 2:
                    dve.wait_ge(w_hi, i + 1)
                    dve.wait_ge(vec_in, 16)
                    for k in range(KC):
                        ins = nc.vector.scalar_tensor_tensor(
                            split_to[i][1][:, k], raw[i][:, k], vec[:, KC * i + k:KC * i + k + 1],
                            split_to[i][0][:, k].bitcast(F32), ALU.mult, ALU.subtract)
                    ins.then_inc(wt_lo, 1)
                elif step == "bias_add":
                    dve.wait_ge(bias_ps, 1)
                    dve.wait_ge(bcst_in, 16)
                    nc.vector.tensor_tensor(bcst[:, 2], bcst[:, 2], ps_p[0:TT, bank["bias", 0]], ALU.add).then_inc(bias_sb, 1)
                elif step == "x_stats":
                    dve.wait_ge(x_in[i % 2], 16 * (i // 2 + 1))
                    moments(0, i, xt[:, i % 2], EPS_TOK)
                elif step == "x_norm":
                    normed(0, i, xt[:, i % 2], xt[:, i % 2]).then_inc(x_norm, 1)
                elif step == "xT_lo":
                    dve.wait_ge(xT_hi, i + 1)
                    part = [w[:, KC * (i % 2):KC * (i % 2 + 1)].rearrange("p k t -> p (k t)") for w in xT]
                    rest(part[1], ps_x[:, i % 2, 0:HT], part[0]).then_inc(xT_lo, 1)
                elif step == "h_stats":
                    dve.wait_ge(h_ps, i + 1)
                    if i == NT - 2:
                        dve.wait_ge(z_out, 16 * (E + 2))
                    if i == 0:
                        dve.wait_ge(bias_sb, 1)
                    nc.vector.tensor_tensor(h2[:, i], ps_p[0:TT, bank["embed", i]], bcst[:, 2], ALU.add).then_inc(h_evac, 1)
                    dve.wait_ge(h_evac, i + 1)
                    moments(1, i, h2[:, i], EPS_TOK)
                elif step == "h_norm":
                    normed(1, i, h2[:, i], h2[:, i]).then_inc(h_norm, 1)
                elif step == "a_stats":
                    dve.wait_ge(h_rdy, i + 1)
                    moments(2, i, h2[:, i], EPS_LN)
                elif step == "a_norm":
                    if i >= 1:
                        dve.wait_ge(aT_ps, i)
                    normed(2, i, an[:], h2[:, i]).then_inc(a_norm, 1)
                elif step == "aT_lo":
                    u = i % HALF
                    dve.wait_ge(aT_hi, i + 1)
                    part = [w[:, :, u * TT:(u + 1) * TT] for w in anT]
                    rest(part[1], ps_t[:, 0:HT].rearrange("p (k t) -> p k t", k=KC), part[0]).then_inc(aT_lo, 1)
                elif step == "qk_elu":
                    dve.wait_ge(e_sb, i + 1)
                    st.done(nc.vector.tensor_scalar(ebuf[:], ebuf[:], 1.0, None, ALU.min))
                    if i == 2 * KC:
                        dve.wait_ge(h_ps, NT)
                    dst = (kTs if i % 2 == 0 else qTs)[i // (2 * KC)][:, i // 2 % KC]
                    nc.vector.scalar_tensor_tensor(dst, ps_p[:, bank["qk", i], 0:HT], 0.0, ebuf[:],
                                                   ALU.max, ALU.add).then_inc(qk_sb, 1)
                elif step == "q_times_sum":
                    g, m = i // KC, i % KC
                    per = lambda a: a.rearrange("p (b s) -> p b s", s=NPATCH)
                    dve.wait_ge(qk_sb, 2 * i + 2)
                    st.done(nc.vector.reduce_sum(ksum[:, m], per(kTs[g][:, m]), AX_X))
                    if i >= 1:
                        dve.wait_ge(den_ps, i)
                    nc.vector.tensor_tensor(per(kq[:]), per(qTs[g][:, m]),
                                            ksum[:, m].unsqueeze(2).to_broadcast([P, HT // NPATCH, NPATCH]),
                                            ALU.mult).then_inc(kq_rdy, 1)
                elif step == "den_inv":
                    dve.wait_ge(den_sb, i + 1)
                    nc.vector.reciprocal(dsb[:], dsb[:]).then_inc(den_inv, 1)
                elif step == "mask":
                    dve.wait_ge(s_ps, i + 1)
                    if i >= 2:
                        dve.wait_ge(n_ps, i - 1)
                    mask = cst[0:TT, CO_MASK:CO_MASK + TT].unsqueeze(1).to_broadcast([TT, HPB, TT])
                    nc.vector.tensor_tensor(ssb[:, i % 2].rearrange("p (h t) -> p h t", h=HPB),
                                            ps_s[0:TT, i % 2, 0:HPB * TT].rearrange("p (h t) -> p h t", h=HPB),
                                            mask, ALU.mult).then_inc(s_sb, 1)
                elif step == "att_lo":
                    dve.wait_ge(att_hi, i + 1)
                    rest(attT[1][:].rearrange("p k t -> p (k t)"), ps_o[:, 0:HT],
                         attT[0][:].rearrange("p k t -> p (k t)")).then_inc(att_lo, 1)
                elif step == "residual":
                    dve.wait_ge(wo_ps, i + 1)
                    nc.vector.tensor_tensor(h2[:, i], h2[:, i], ps_p[0:TT, bank["project", i]], ALU.add).then_inc(h2_rdy, 1)
                    dve.wait_ge(h2_rdy, i + 1)
                    moments(3, i, h2[:, i], EPS_LN)
                elif step == "t_norm":
                    if i >= 1:
                        dve.wait_ge(tT_ps, i)
                    normed(3, i, tn[:], h2[:, i]).then_inc(t_norm, 1)
                elif step == "gate_copy":
                    dve.wait_ge(g_ps, i + 1)
                    nc.vector.tensor_copy(logits[:, i], ps_p[0:TT, bank["gate", i], 0:E]).then_inc(lg_sb, 1)

            dve.wait_ge(lg_sb, NT)
            nc.vector.tensor_copy(trib[:], cst[0:TT, CO_TRI:CO_TRI + 2 * TT])
            t3 = lambda n: rt[:, n].rearrange("p (t e) -> p t e", e=E)
            per_e = lambda a: a.unsqueeze(2).to_broadcast([TT, NT, E])
            st.done(nc.vector.reduce_max(rs[:, 0], logits[:], AX_X))
            nc.vector.tensor_tensor(t3(0), logits[:], per_e(rs[:, 0]), ALU.subtract).then_inc(r_diff, 1)
            st.done(nc.vector.tensor_tensor(t3(2), logits[:], per_e(rs[:, 0]), ALU.is_equal))
            st.done(nc.vector.tensor_tensor(rt[:, 3], rt[:, 2], cst[0:TT, CO_REV:CO_REV + NT * E], ALU.mult))
            st.done(nc.vector.reduce_max(rs[:, 1], t3(3), AX_X))
            st.done(nc.vector.tensor_tensor(t3(4), t3(3), per_e(rs[:, 1]), ALU.is_equal))
            nc.vector.tensor_copy(ohb[:], rt[:, 4]).then_inc(r_oh, 1)

            def again(t):
                return nc.vector.tensor_scalar(rows[:, t], h2[:, t], mv[:, 3, t, 0:1], rstd[:, 3, t:t + 1],
                                               ALU.subtract, ALU.mult)

            for t in range(2):
                again(t).then_inc(rows_rdy, 1)
            st.done(nc.vector.tensor_tensor(rt[:, 5], rt[:, 4], cst[0:TT, CO_OFF:CO_OFF + NT * E], ALU.mult))
            st.done(nc.vector.reduce_sum(rs[:, 2], t3(5), AX_X))
            dve.wait_ge(r_ps, 1)
            st.done(nc.vector.tensor_tensor(rt[:, 6], rt[:, 4], ps_p[0:TT, 0, 0:NT * E], ALU.mult))
            st.done(nc.vector.reduce_sum(rs[:, 5], t3(6), AX_X))
            st.done(nc.vector.tensor_scalar(rs[:, 6], rs[:, 5], float(CAP), None, ALU.is_lt))
            st.done(nc.vector.tensor_tensor(rs[:, 7], rs[:, 5], rs[:, 2], ALU.add))
            st.done(nc.vector.tensor_tensor(rs[:, 0], rs[:, 7], cst[0:TT, CO_TOK:CO_TOK + NT], ALU.subtract))
            st.done(nc.vector.tensor_tensor(rs[:, 1], rs[:, 0], rs[:, 6], ALU.mult))
            st.done(nc.vector.tensor_tensor(rs[:, 2], rs[:, 1], cst[0:TT, CO_TOK:CO_TOK + NT], ALU.add))
            nc.vector.tensor_copy(dst_idx[:], rs[:, 2]).then_inc(idx_rdy, 1)
            for t in range(2, NT):
                again(t).then_inc(rows_rdy, 1)
            st.done(nc.vector.tensor_scalar(rs[:, 3], rs[:, 7], float(CAP), None, ALU.add))
            st.done(nc.vector.tensor_tensor(rs[:, 4], rs[:, 3], rs[:, 6], ALU.mult))
            nc.vector.tensor_copy(src_idx[:], rs[:, 4]).then_inc(idx_rdy, 1)
            dve.wait_ge(r_exp, 1)
            st.done(nc.vector.reduce_sum(rs[:, 3], t3(1), AX_X))
            st.done(nc.vector.reciprocal(rs[:, 4], rs[:, 3]))
            nc.vector.tensor_tensor(prob[:], rs[:, 4], rs[:, 6], ALU.mult)
            nc.vector.memset(eT[:], 0.0).then_inc(eT_rdy, 1)

            dve.wait_ge(rowT_ps, 1)
            nc.vector.tensor_copy(xTe[:, 0].rearrange("p (b k) t -> p b (k t)", b=2),
                                  ps_s[:, :, 0:2 * CAP]).then_inc(rowT_sb, 1)
            with dve.Fori(0, E // 2) as i:
                for q in range(2):
                    e = 2 * i + q
                    dve.wait_ge(oT_ps, e + 1)
                    dve.wait_ge(eo_free, e + 1)
                    nc.vector.tensor_copy(eorow[:, 1 - q], ps_s[0:CH, :, :]).then_inc(eo_rdy, 1)
                    dve.wait_ge(rowT_ps, e + 2)
                    nc.vector.tensor_copy(xTe[:, 1 - q].rearrange("p (b k) t -> p b (k t)", b=2),
                                          ps_s[:, :, 0:2 * CAP]).then_inc(rowT_sb, 1)
                    dve.wait_ge(ew_ps, WP * (e + 1))
                    for b in range(2):
                        ins = nc.vector.tensor_copy(eT[:, q, 2 * b:2 * b + 2].rearrange("p k t -> p (k t)"),
                                                    ps_e[b][:, 0:2 * CAP])
                    ins.then_inc(eT_rdy, 1)
            dve.wait_ge(oT_ps, E + 1)
            dve.wait_ge(eo_free, E + 1)
            nc.vector.tensor_copy(eorow[:, (E - 1) % 2], ps_s[0:CH, :, :]).then_inc(eo_rdy, 1)
            for t in range(NT):
                dve.wait_ge(gath[t], 16)
                nc.vector.scalar_tensor_tensor(h2[:, t], rows[:, t], prob[:, t:t + 1], h2[:, t],
                                               ALU.mult, ALU.add).then_inc(o_rdy, 1)

        @block.tensor
        def _(pe):
            def mm(o, a, b, first, last, **kw):
                return nc.tensor.matmul(o, a, b, start=first, stop=last, **kw)

            def mm3(o, a, b, first, last):
                mm(o, a[0], b[0], first, False)
                mm(o, a[0], b[1], False, False)
                return mm(o, a[1], b[0], False, last)

            def of(pair, *at_):
                return [w[at_] for w in pair]

            def free(table, key):
                if table[key]:
                    pe.wait_ge(*table[key])

            every = slice(None)
            pe.wait_ge(c_in, 16)
            for step, i in schedule:
                if step == "bias":
                    pe.wait_ge(w_in[0], 16)
                    pe.wait_ge(w_in[1], 16)
                    pe.wait_ge(vec_in, 16)
                    for k in range(KX):
                        ins = mm(ps_p[0:TT, bank[step, i]], vec[:, KX + k:KX + k + 1].to_broadcast([P, TT]),
                                 raw[k // KC][:, k % KC], k == 0, k == KX - 1)
                    ins.then_inc(bias_ps, 1)
                elif step == "x_turn":
                    pe.wait_ge(x_norm, i + 1)
                    if i >= 1:
                        pe.wait_ge(xT_lo, 2 * i)
                    for k in range(KX):
                        ins = nc.tensor.transpose(ps_x[:, k // 4, (k % 4) * TT:(k % 4 + 1) * TT],
                                                  xt[:, i % 2, k * P:(k + 1) * P], ident[0:TT, 0:TT])
                    ins.then_inc(xT_ps, 1)
                elif step == "embed":
                    if i == 0:
                        pe.wait_ge(wt_lo, 2)
                    free(before, (step, i))
                    for b, done in enumerate((h_mid, h_ps)):
                        pe.wait_ge(xT_lo, 2 * i + b + 1)
                        for k in range(KC * b, KC * (b + 1)):
                            ins = mm3(ps_p[0:TT, bank[step, i]], of(xT, every, k), of(wtok, every, k), k == 0, k == KX - 1)
                        ins.then_inc(done, 1)
                elif step == "a_turn":
                    pe.wait_ge(a_norm, i + 1)
                    free(before_t, (step, i))
                    for k in range(KC):
                        ins = nc.tensor.transpose(ps_t[:, k * TT:(k + 1) * TT], an[:, k * P:(k + 1) * P], ident[0:TT, 0:TT])
                    ins.then_inc(aT_ps, 1)
                elif step == "v":
                    u = i % HALF
                    pe.wait_ge(aT_lo, i + 1)
                    if i == 0:
                        pe.wait_ge(w_lo, 1)
                    free(before, (step, i))
                    for k in range(KC):
                        ins = mm3(ps_p[0:TT, bank[step, i]], of(anT, every, k, slice(u * TT, (u + 1) * TT)),
                                  of(wvs, every, k), k == 0, k == KC - 1)
                    ins.then_inc(v_ps, 1)
                elif step == "qk":
                    w, m = (wks, wqs)[i % 2], i // 2 % KC
                    if i % (2 * KC) == 0:
                        pe.wait_ge(aT_lo, HALF * (i // (2 * KC) + 1))
                        pe.wait_ge(w_lo, 3)
                    free(before, (step, i))
                    for k in range(KC):
                        ins = mm3(ps_p[:, bank[step, i], 0:HT], of(w, every, k, slice(m * P, (m + 1) * P)),
                                  of(anT, every, k), k == 0, k == KC - 1)
                    ins.then_inc(qk_ps, 1)
                elif step == "den":
                    pe.wait_ge(kq_rdy, i + 1)
                    free(before, (step, i))
                    mm(ps_p[:, bank[step, i], 0:HT], cst[:, CO_BLK:CO_BLK + P], kq[:], True, True).then_inc(den_ps, 1)
                elif step == "scores":
                    u, m = i // KC % HALF, i % KC
                    pe.wait_ge(qb_rdy, i + 1)
                    if i >= 2:
                        pe.wait_ge(s_sb, i - 1)
                    mm(ps_s[0:TT, i % 2, 0:HPB * TT], kTs[i // (HALF * KC)][:, m, u * TT:(u + 1) * TT], qblk[:, i % 2],
                       True, True).then_inc(s_ps, 1)
                elif step == "attend":
                    u, m = i // KC % HALF, i % KC
                    pe.wait_ge(s_sb, i + 1)
                    if m == 0:
                        pe.wait_ge(v_sb, i // KC + 1)
                    if m == 0 and i >= KC:
                        pe.wait_ge(att_lo, i // KC)
                    for h in range(HPB):
                        ins = mm(ps_o[DH * h:DH * (h + 1), m * TT:(m + 1) * TT],
                                 vsb[:, i // KC, m * P + DH * h:m * P + DH * (h + 1)],
                                 ssb[:, i % 2, h * TT:(h + 1) * TT], True, True)
                    ins.then_inc(n_ps, 1)
                elif step == "project":
                    pe.wait_ge(att_lo, i + 1)
                    if i == 0:
                        pe.wait_ge(w_lo, 4)
                    free(before, (step, i))
                    for k in range(KC):
                        ins = mm3(ps_p[0:TT, bank[step, i]], of(attT, every, k), of(wos, every, k), k == 0, k == KC - 1)
                    ins.then_inc(wo_ps, 1)
                elif step == "t_turn":
                    pe.wait_ge(t_norm, i + 1)
                    free(before_t, (step, i))
                    for k in range(KC):
                        ins = nc.tensor.transpose(ps_t[:, k * TT:(k + 1) * TT], tn[:, k * P:(k + 1) * P], ident[0:TT, 0:TT])
                    ins.then_inc(tT_ps, 1)
                elif step == "gate":
                    pe.wait_ge(tT_sb, i + 1)
                    if i == 0:
                        pe.wait_ge(gate_in, 16)
                    free(before, (step, i))
                    for k in range(KC):
                        ins = mm(ps_p[0:TT, bank[step, i], 0:E], t2T[:, k], gsb[:, k], k == 0, k == KC - 1)
                    ins.then_inc(g_ps, 1)

            pe.wait_ge(r_oh, 1)
            pe.wait_ge(lg_sb, NT)
            for d in range(NT):
                ins = mm(ps_p[0:TT, 0, E * d:E * NT], trib[:, TT * min(d, 1):TT * (min(d, 1) + 1)],
                         ohb[:, 0:E * (NT - d)], d == 0, d == NT - 1, skip_group_check=True)
            ins.then_inc(r_ps, 1)

            def slots_turned(e, q):
                pe.wait_ge(xrow_in[q], 8 * (e - q) + 16)
                for k in range(KC):
                    for c in range(2):
                        ins = nc.tensor.transpose(
                            ps_s[:, k // 2, (k % 2) * CAP + c * CH:(k % 2) * CAP + (c + 1) * CH],
                            xrow[:, q, c, k * P:(k + 1) * P], ident[0:CH, 0:CH])
                ins.then_inc(rowT_ps, 1)

            def outputs_turned(e, q):
                for c in range(2):
                    for m in range(KC):
                        ins = nc.tensor.transpose(ps_s[0:CH, c, m * P:(m + 1) * P],
                                                  eT[:, q, m, c * CH:(c + 1) * CH], ident)
                ins.then_inc(oT_ps, 1)

            slots_turned(0, 0)
            pe.wait_ge(idx_rdy, 1)
            with pe.Fori(0, E // 2) as i:
                for q in range(2):
                    e = 2 * i + q
                    for j in range(WP):
                        s = q * PIECES + j
                        pe.wait_ge(slot_in[s], 16 * i + 16)
                        if j == 0:
                            pe.wait_ge(rowT_sb, e + 1)
                        if j >= 2:
                            pe.wait_ge(g_sb, WP * e + j - 1)
                        for c in range(4):
                            for k in range(KC):
                                ins = mm(ps_h[j % 2][:, c // 2, (c % 2) * CAP:(c % 2 + 1) * CAP],
                                         ring[s][:, k, c * P:(c + 1) * P], xTe[:, q, k], k == 0, k == KC - 1)
                        ins.then_inc(hm_ps, 1)
                        if j == 1:
                            pe.wait_ge(eT_rdy, e + 1)
                            outputs_turned(e - 1, 1 - q)
                        if j == 3:
                            pe.wait_ge(eo_rdy, e + 1)
                            slots_turned(e + 1, 1 - q)
                    for j in range(WP):
                        s = q * PIECES + WP + j
                        pe.wait_ge(slot_in[s], 16 * i + 16)
                        pe.wait_ge(g_sb, WP * e + j + 1)
                        for b in range(4):
                            for m in range(KC):
                                ins = mm(ps_e[m // 2][:, (m % 2) * CAP:(m % 2 + 1) * CAP],
                                         ring[s][:, b, m * P:(m + 1) * P], hmT[:, q, 4 * j + b],
                                         j == 0 and b == 0 and m % 2 == 0, j == WP - 1 and b == 3,
                                         skip_group_check=True)
                        ins.then_inc(ew_ps, 1)
                    pe.wait_ge(rowT_sb, e + 2)
            pe.wait_ge(eT_rdy, E + 1)
            outputs_turned(E - 1, (E - 1) % 2)


def kernel(x, L0_tok_W, L0_tok_b, L0_tok_g1, L0_tok_b1, L0_tok_g2, L0_tok_b2, L0_attn_cos, L0_attn_sin,
           L0_attn_Wq, L0_attn_Wk, L0_attn_Wv, L0_attn_Wo, L0_ffn_gate_weight, L0_ffn_wi, L0_ffn_wo):
    import concourse.bacc as bacc
    from concourse.bass_utils import run_bass_kernel_spmd

    a = np.asarray
    t = lambda w: np.ascontiguousarray(a(w).T)
    by_partition = lambda v: a(v).reshape(KX, P).T
    ins = {
        "x": np.ascontiguousarray(a(x)[:, :NPATCH * TIN]).reshape(TOKENS, IN_DIM),
        "w_tok": a(L0_tok_W),
        "cols": np.ascontiguousarray(np.concatenate([by_partition(L0_tok_g1), by_partition(L0_tok_b1)], 1)),
        "g2b2b": np.stack([a(L0_tok_g2), a(L0_tok_b2), a(L0_tok_b)]),
        "wq": t(L0_attn_Wq), "wk": t(L0_attn_Wk), "wv": t(L0_attn_Wv), "wo": t(L0_attn_Wo),
        "gate": t(L0_ffn_gate_weight),
        "wi": a(L0_ffn_wi), "wout": a(L0_ffn_wo),
        "consts": constants(),
    }
    nc = bacc.Bacc("TRN2", target_bir_lowering=False, num_devices=1)
    args = {n: nc.dram_tensor(f"in_{n}", v.shape, F32, kind="ExternalInput").ap() for n, v in ins.items()}
    args["out"] = nc.dram_tensor("out_0", (TOKENS, C), F32, kind="ExternalOutput").ap()
    audio_tower(nc, **args)
    r = run_bass_kernel_spmd(nc, [{f"in_{n}": v for n, v in ins.items()}], core_ids=[0])
    return r.results[0]["out_0"].reshape(BATCH, NPATCH, C)
```

```python
from contextlib import ExitStack

import numpy as np
import concourse.bass as bass
from concourse import mybir

F32 = mybir.dt.float32
F32R = mybir.dt.float32r
BF16 = mybir.dt.bfloat16
U32 = mybir.dt.uint32
ALU = mybir.AluOpType
ACT = mybir.ActivationFunctionType
AX_X = mybir.AxisListType.X

P = 128
BATCH, SEQ, FEAT = 64, 250, 64
TIN = 16
NPATCH = SEQ // TIN
IN_DIM = TIN * FEAT
C = 512
TOKENS = BATCH * NPATCH
BT = 8
TT = BT * NPATCH
NT = TOKENS // TT
HALF = NT // 2
HT = HALF * TT
GROUPS = ((0, 6), (6, NT))
KX = IN_DIM // P
KC = C // P
DH = 32
HPB = P // DH
E = 8
INTER = 2048
KI = INTER // P
CAP = TOKENS * 5 // 4 // E
CH = CAP // 2
REST = CAP - P
BLOCKS = KI
WB = 4
EPS_TOK, EPS_LN, EPS_Z = 1e-6, 1e-5, 1e-6

PIECES = 8
WP = PIECES // 2
SLOTS = 2 * PIECES

XS_ROWS = (E + 2) * CAP
EO_ROWS = 1 + E * CAP

EMBED_AT = (-27.2, -12.3, 3.3, 15.8, 33.4, 45.0, 62.3, 85.8)
EMBED = {
    "x_stats": (-31.8, -31.8), "x_root": (-24.6, -24.6), "x_norm": (-19.8, -19.8), "x_turn": (-4.6, -4.6),
    "embed": (6.7, 6.7), "h_stats": (3.2, 3.2), "h_root": (7.8, 7.8), "h_norm": (8.7, 8.7),
    "h_affine": (13.7, 13.7), "a_stats": (14.3, 16.4), "a_root": (19.0, 26.7), "a_norm": (16.6, 25.9),
    "a_turn": (32.0, 38.6), "aT_hi": (33.0, 38.7), "aT_lo": (27.4, 37.8), "v": (42.2, 52.3), "v_copy": (39.1, 48.1),
}
XT_EACH = 1.1
XT = {"xT_hi": -7.8, "xT_lo": -8.4}
QK_AT = ((50.9, 55.8, 64.8, 71.4),
         (130.7, 146.9, 172.3, 198.5))
QK_EACH = 2.5
QK = {"qk": 2.7, "qk_exp": 0.4, "qk_elu": -0.6}
DEN = {"q_times_sum": 5.4, "den": 15.9, "den_copy": 13.8, "den_inv": 12.9, "q_div": 17.3}
ATTEND_AT = (93.3, 119.4, 147.2, 183.7, 215.9, 247.0, 276.4, 304.9)
BLOCK_EACH = 6.78
BLOCK = {"q_blocks": -18.2, "scores": -2.4, "mask": -6.0, "attend": 9.4}
ATTENDED = {
    "att_hi": -0.9, "att_lo": -2.6, "project": 10.0, "residual": 6.9, "t_root": 16.3, "t_norm": 24.7,
    "t_turn": 36.1, "tT_copy": 42.3, "gate": 53.3, "gate_copy": 45.3,
}
WEIGHTS_AT = (-44.7, -40.7, -23.3, -5.1, 30.1, 34.1)
ROUTE_AT = (338.1, 386.3)
ROUTE = {"pick": 0, "rank": 20.0, "place": 25.8}
SEND, SEND_EACH = (25.3, 25.3), 0.1
BIAS_AT, BIAS_ADD_AT = -31.5, -24.7


def front_schedule():
    order = []
    for t in range(NT):
        order += [(EMBED_AT[t] + lag[t // HALF], step, t) for step, lag in EMBED.items()]
        for b in range(2):
            order += [(EMBED_AT[t] + XT_EACH * b + lag, step, 2 * t + b) for step, lag in XT.items()]
        for m in range(KC):
            order += [(ATTEND_AT[t] + BLOCK_EACH * m + lag, step, KC * t + m) for step, lag in BLOCK.items()]
        order += [(ATTEND_AT[t] + BLOCK_EACH * KC + lag, step, t) for step, lag in ATTENDED.items()]
    for b in range(2 * KC):
        at = QK_AT[b // KC][b % KC]
        for j in range(2):
            order += [(at + QK_EACH * j + lag, step, 2 * b + j) for step, lag in QK.items()]
        order += [(at + lag, step, b) for step, lag in DEN.items()]
    for g, (first, end) in enumerate(GROUPS):
        order += [(ROUTE_AT[g] + lag, step, g) for step, lag in ROUTE.items()]
        for t in range(first, end):
            at = ROUTE_AT[g] + SEND[g] + SEND_EACH * (t - first)
            order += [(at, "row", t), (at + 0.1, "send", t)]
    for n in range(6):
        order += [(WEIGHTS_AT[n], "w_hi", n), (WEIGHTS_AT[n] + 0.1, "w_lo", n)]
    order += [(BIAS_AT, "bias", 0), (BIAS_ADD_AT, "bias_add", 0)]
    order = [(step, i) for _, step, i in sorted(order)]
    for kind in {step for step, _ in order}:
        turns = [i for step, i in order if step == kind]
        assert turns == sorted(turns), kind
    return order


CO_ID = 0
CO_BLK = CO_ID + P
CO_MASK = CO_BLK + P
CO_TRI = CO_MASK + TT
CO_HM = CO_TRI + TT
CO_REV = CO_HM + HPB
CO_OFF = CO_REV + NT * E
CO_TOK = CO_OFF + NT * E
CO_N = CO_TOK + NT


def constants():
    c = np.zeros((P, CO_N), np.float32)
    r = np.arange(P)
    c[:, CO_ID:CO_ID + P] = np.eye(P)
    c[:, CO_BLK:CO_BLK + P] = r[:, None] // DH == r[None] // DH
    s = np.arange(TT)
    c[:TT, CO_MASK:CO_MASK + TT] = s[:, None] // NPATCH == s[None] // NPATCH
    c[:TT, CO_TRI:CO_TRI + TT] = s[:, None] < s[None]
    c[:, CO_HM:CO_HM + HPB] = r[:, None] // DH == np.arange(HPB)[None]
    c[:, CO_REV:CO_REV + NT * E] = np.tile(E - np.arange(E), NT)
    c[:, CO_OFF:CO_OFF + NT * E] = np.tile(CAP * np.arange(E), NT)
    c[:TT, CO_TOK:CO_TOK + NT] = XS_ROWS + s[:, None] + TT * np.arange(NT)[None]
    return c


def audio_tower(nc, x, w_tok, cols, g2b2b, wq, wk, wv, wo, gate, wi, wout, consts, out):
    xs_dram = nc.dram_tensor("xs_rows", (XS_ROWS + TOKENS, C), F32).ap()
    eo_dram = nc.dram_tensor("eo_rows", (EO_ROWS, C), F32).ap()

    with ExitStack() as ctx:
        def psum(name, shape):
            return ctx.enter_context(nc.psum_tensor(name, shape, F32))

        def sem(name):
            return ctx.enter_context(nc.semaphore(name))

        start = (nc.sbuf_base + 63) // 64 * 64
        size = (nc.sbuf_bytes_remaining - 128) // 64 * 64
        ctx.enter_context(nc.sbuf_tensor("arena", [P, size], mybir.dt.uint8))
        at = [start]

        def place(name, shape, dt=F32):
            n = int(np.prod(shape[1:])) * (2 if dt == BF16 else 4)
            t = nc.alloc_sbuf_tensor_at(name, shape, dt, offset=at[0])
            at[0] += (n + 31) // 32 * 32
            assert at[0] <= start + size, (name, at[0] - start - size)
            return t

        def halves(name, shape):
            return place(name + "_hi", shape, F32R), place(name + "_lo", shape, F32R)

        cst = place("cst", [P, CO_N])
        h2 = place("h2", [TT, NT, C])
        logits = place("logits", [TT, NT, E])
        prob = place("prob", [TT, NT])
        src_idx = place("src_idx", [TT, NT], U32)
        counts = place("counts", [1, E], mybir.dt.int32)
        rt = place("rt", [TT, 3, NT * E])
        rs = place("rs", [TT, 6, NT])
        ohb = place("ohb", [TT, NT * E], BF16)
        trib = place("trib", [TT, 2 * TT], BF16)
        dst_idx = place("dst_idx", [TT, NT], U32)
        shared = at[0]

        wvs = halves("wv", [P, KC, C])
        wks, wqs = halves("wk", [P, KC, C]), halves("wq", [P, KC, C])
        wtok_at = at[0]
        wtok = halves("wtok", [P, KX, C])
        end, at[0] = at[0], wtok_at + 4 * KX * C
        kT1, qT1 = place("kT1", [P, KC, HT]), place("qT1", [P, KC, HT])
        assert at[0] <= end
        at[0] = end
        wos = halves("wo", [P, KC, C])
        rows_at = at[0]
        xt = place("xt", [TT, 2, IN_DIM])
        xT = halves("xT", [P, KX, TT])
        an = place("an", [TT, C])
        end, at[0] = at[0], rows_at
        rows = place("rows", [TT, NT, C])
        assert at[0] <= end
        at[0] = end
        bcst = place("bcst", [TT, 3, C])
        vec = place("vec", [P, 2 * KX])
        gsb = place("gsb", [P, KC, E])
        mv = place("mv", [TT, 4, NT, 2])
        rstd = place("rstd", [TT, 4, NT])
        stats = place("stats", [TT, 4, 2, 6])
        std = place("std", [TT, 4, NT])
        ksum = place("ksum", [P, HT // NPATCH])
        anT = halves("anT", [P, KC, HT])
        tn = place("tn", [TT, C])
        stage_at = at[0]
        kTs, qTs = [place("kT0", [P, KC, HT]), kT1], [place("qT0", [P, KC, HT]), qT1]
        kq = place("kq", [P, HT])
        dsb = place("dsb", [P, HT])
        ebuf = place("ebuf", [P, HT])
        qblk = place("qblk", [P, 2, HPB * TT])
        ssb = place("ssb", [TT, 2, HPB * TT])
        attT = halves("attT", [P, KC, TT])
        t2T = place("t2T", [P, KC, TT])
        vsb = place("vsb", [TT, NT, C])
        end, at[0] = at[0], stage_at
        raw = [place(f"raw{s}", [P, KC, C]) for s in range(3)]
        assert at[0] <= end - 4 * NT * C, "the staging reaches into vsb"

        at[0] = shared
        ring = [place(f"ring{s}", [P, KC, C]) for s in range(SLOTS)]
        xrow = place("xrow", [CH, 2, 2, C])
        xTe = place("xTe", [P, 2, KC, CAP])
        eorow = place("eorow", [P, 2, C])
        eorest = place("eorest", [P, 2, P])
        hms = halves("hm", [P, KI, P])
        wouts = halves("wout", [P, WB, C])
        hmT = place("hmT", [P, KI, CAP])

        ident = cst[:, CO_ID:CO_ID + P]

        ps_x = psum("ps_x", [P, 2, 512])
        ps_p = psum("ps_p", [P, 2, 512])
        ps_t = psum("ps_t", [P, 512])
        ps_o = psum("ps_o", [P, 512])
        ps_s = psum("ps_s", [P, 2, 512])
        ps_h = [ps_x, ps_p]

        c_in, vec_in, bcst_in, gate_in = sem("c_in"), sem("vec_in"), sem("bcst_in"), sem("gate_in")
        z_out, z_set = sem("z_out"), sem("z_set")
        w_in = [sem(f"w_in{n}") for n in range(6)]
        x_in = [sem(f"x_in{u}") for u in range(2)]
        slot_in = [sem(f"slot_in{s}") for s in range(SLOTS)]
        scat, y_out, eo_out = sem("scat"), sem("y_out"), [sem("eo_out0"), sem("eo_out1")]
        xrow_in = [sem("xrow_in0"), sem("xrow_in1")]
        gath = [sem(f"gath{t}") for t in range(NT)]
        bias_ps, bias_sb, w_hi, w_lo = sem("bias_ps"), sem("bias_sb"), sem("w_hi"), sem("w_lo")
        wt_lo, h_mid = sem("wt_lo"), sem("h_mid")
        mv_rdy, std_rdy = [sem(f"mv_rdy{r}") for r in range(4)], [sem(f"std_rdy{r}") for r in range(4)]
        x_norm, xT_ps, xT_hi, xT_lo, h_ps, h_evac, h_norm, h_mul, h_rdy = (sem(n) for n in (
            "x_norm", "xT_ps", "xT_hi", "xT_lo", "h_ps", "h_evac", "h_norm", "h_mul", "h_rdy"))
        a_norm, aT_ps, aT_hi, aT_lo, v_ps, v_sb, qk_ps, e_sb, qk_sb = (sem(n) for n in (
            "a_norm", "aT_ps", "aT_hi", "aT_lo", "v_ps", "v_sb", "qk_ps", "e_sb", "qk_sb"))
        kq_rdy, den_ps, den_sb, den_inv, qn_rdy, qb_rdy, s_ps, s_sb, n_ps, att_hi, att_lo = (sem(n) for n in (
            "kq_rdy", "den_ps", "den_sb", "den_inv", "qn_rdy", "qb_rdy", "s_ps", "s_sb", "n_ps", "att_hi", "att_lo"))
        wo_ps, h2_rdy, t_norm, tT_ps, tT_sb, g_ps, lg_sb = (sem(n) for n in (
            "wo_ps", "h2_rdy", "t_norm", "tT_ps", "tT_sb", "g_ps", "lg_sb"))
        dve_step = sem("dve_step")
        r_diff, r_exp, src_rdy, r_oh, r_ps, idx_rdy = (sem(n) for n in (
            "r_diff", "r_exp", "src_rdy", "r_oh", "r_ps", "idx_rdy"))
        rows_rdy, counts_rdy, rank_read = sem("rows_rdy"), sem("counts_rdy"), sem("rank_read")
        rowT_ps, rowT_sb, hm_ps, g_sb, hm_hi, hm_lo, eo_rdy, o_rdy = (sem(n) for n in (
            "rowT_ps", "rowT_sb", "hm_ps", "g_sb", "hm_hi", "hm_lo", "eo_rdy", "o_rdy"))
        wo_hi, wo_lo, wo_used = sem("wo_hi"), sem("wo_lo"), sem("wo_used")

        block = ctx.enter_context(nc.Block())

        x_t = x.rearrange("(t p) d -> t p d", p=TT)
        out_t = out.rearrange("(t p) d -> t p d", p=TT)
        wi_v = wi.rearrange("(i q) (k p) (j n) -> i q j p k n", q=2, p=P, n=C)
        wo_v = wout.rearrange("(i q) (j k p) n -> i q j p k n", q=2, p=P, k=KC)
        xs_v = xs_dram[0:XS_ROWS].rearrange("(i q c p) d -> i q p c d", q=2, c=2, p=CH)
        eo_v = eo_dram[1:EO_ROWS].rearrange("(i q p) d -> i q p d", q=2, p=CAP)
        by_block = lambda w: w.rearrange("(k p) n -> p k n", p=P)
        weights = [by_block(w_tok)[:, 0:KC], by_block(w_tok)[:, KC:KX],
                   by_block(wv), by_block(wk), by_block(wq), by_block(wo)]
        split_to = [tuple(w[:, 0:KC] for w in wtok), tuple(w[:, KC:KX] for w in wtok), wvs, wks, wqs, wos]

        EO_COUNT = 16 * (1 + KC)
        schedule = front_schedule()
        read_by = {"bias": bias_sb, "embed": h_evac, "v": v_sb, "qk": qk_sb, "den": den_sb,
                   "project": h2_rdy, "gate": lg_sb, "rank": rank_read}
        uses = [step for step in schedule if step[0] in read_by]
        bank = {step: n % 2 for n, step in enumerate(uses)}
        before = {step: (read_by[uses[n - 2][0]], uses[n - 2][1] + 1) if n >= 2 else None
                  for n, step in enumerate(uses)}
        turned = [step for step in schedule if step[0] in ("a_turn", "t_turn")]
        before_t = {step: ((aT_lo if turned[n - 1][0] == "a_turn" else tT_sb), turned[n - 1][1] + 1) if n else None
                    for n, step in enumerate(turned)}

        class Steps:

            def __init__(self, eng):
                self.eng, self.n = eng, 0

            def done(self, ins):
                self.n += 1
                ins.then_inc(dve_step, 1)
                self.eng.wait_ge(dve_step, self.n)

        @block.sync
        def _(sp):
            def load_w(n):
                sp.dma_start(raw[n % 3][:], weights[n]).then_inc(w_in[n], 16)

            sp.dma_start(xt[:, 0], x_t[0]).then_inc(x_in[0], 16)
            sp.dma_start(vec[:], cols).then_inc(vec_in, 16)
            sp.dma_start(cst[:], consts).then_inc(c_in, 16)
            load_w(0)
            load_w(1)
            sp.dma_start(xt[:, 1], x_t[1]).then_inc(x_in[1], 16)
            sp.dma_start(bcst[:], g2b2b.partition_broadcast(TT)).then_inc(bcst_in, 16)
            load_w(2)
            sp.dma_start(gsb[:], gate.rearrange("(k p) e -> p k e", p=P)).then_inc(gate_in, 16)
            for t in range(2, NT):
                sp.wait_ge(xT_ps, t - 1)
                sp.dma_start(xt[:, t % 2], x_t[t]).then_inc(x_in[t % 2], 16)
                if t < 5:
                    n = t + 1
                    if n < 5:
                        sp.wait_ge(wt_lo, n - 2)
                        sp.wait_ge(bias_ps, 1)
                    else:
                        sp.wait_ge(w_lo, 1)
                    load_w(n)
            sp.wait_ge(z_set, 1)
            z = h2[0:CH, NT - 2:NT].rearrange("p c d -> p (c d)")
            for e in range(E + 2):
                sp.dma_start(xs_v[e // 2, e % 2], z.rearrange("p (c d) -> p c d", c=2)).then_inc(z_out, 16)
            sp.dma_start(eo_dram[0:1], z[0:1, 0:C]).then_inc(z_out, 16)

            def piece(i, s):
                q, j = s // PIECES, s % PIECES
                src = wi_v[i, q, j] if j < WP else wo_v[i, q, j - WP]
                sp.dma_start(ring[s][:], src).then_inc(slot_in[s], 16)

            sp.wait_ge(v_ps, NT)
            for s in range(0, 2):
                piece(0, s)
            sp.wait_ge(qk_ps, 4 * KC)
            for s in range(2, 6):
                piece(0, s)
            sp.wait_ge(h_ps, NT)
            for s in range(6, 8):
                piece(0, s)
            sp.wait_ge(scat, 16 * NT)
            for q in range(2):
                sp.dma_start(xrow[:, q], xs_v[0, q]).then_inc(xrow_in[q], 16)
            for s in range(8, SLOTS):
                piece(0, s)
            with sp.Fori(1, E // 2) as i:
                for s in range(SLOTS):
                    q, j = s // PIECES, s % PIECES
                    n = 2 * WP * i + (q * WP + j % WP + 1 - 2 * WP)
                    if j < WP:
                        sp.wait_ge(hm_ps, n)
                    else:
                        sp.wait_ge(wo_used, BLOCKS // WP * n + WB)
                    piece(i, s)
            for t in range(NT):
                sp.wait_ge(o_rdy, t + 1)
                sp.dma_start(out_t[t], h2[:, t]).then_inc(y_out, 16)
            sp.wait_ge(y_out, 16 * NT)

        @block.gpsimd
        def _(pool):
            nc.gpsimd.memset(h2[:, NT - 2:NT], 0.0).then_inc(z_set, 1)
            pool.wait_ge(c_in, 16)
            pool.wait_ge(bcst_in, 16)
            for step, i in schedule:
                if step == "h_affine":
                    pool.wait_ge(h_norm, i + 1)
                    nc.gpsimd.tensor_tensor(h2[:, i], h2[:, i], bcst[:, 0], ALU.mult).then_inc(h_mul, 1)
                    pool.wait_ge(h_mul, i + 1)
                    nc.gpsimd.tensor_tensor(h2[:, i], h2[:, i], bcst[:, 1], ALU.add).then_inc(h_rdy, 1)
                elif step == "w_lo" and i >= 2:
                    pool.wait_ge(w_hi, i + 1)
                    nc.gpsimd.tensor_tensor(split_to[i][1][:], raw[i % 3][:], split_to[i][0][:].bitcast(F32),
                                            ALU.subtract).then_inc(w_lo, 1)
                elif step == "q_div":
                    pool.wait_ge(den_inv, i + 1)
                    qm = qTs[i // KC][:, i % KC]
                    nc.gpsimd.tensor_tensor(qm, qm, dsb[:], ALU.mult).then_inc(qn_rdy, 1)
                elif step == "q_blocks":
                    g, u, m = i // (HALF * KC), i // KC % HALF, i % KC
                    pool.wait_ge(qn_rdy, KC * g + m + 1)
                    if i >= 2:
                        pool.wait_ge(s_ps, i - 1)
                    q4 = qTs[g][:, m, u * TT:(u + 1) * TT].unsqueeze(1).to_broadcast([P, HPB, TT])
                    hm4 = cst[:, CO_HM:CO_HM + HPB].unsqueeze(2).to_broadcast([P, HPB, TT])
                    nc.gpsimd.tensor_tensor(qblk[:, i % 2].rearrange("p (h t) -> p h t", h=HPB),
                                            q4, hm4, ALU.mult).then_inc(qb_rdy, 1)
                elif step == "send":
                    g = [first <= i < end for first, end in GROUPS].index(True)
                    pool.wait_ge(idx_rdy, g + 1)
                    pool.wait_ge(rows_rdy, i + 1)
                    if i == 0:
                        pool.wait_ge(z_out, 16 * (E + 3))
                    pool.indirect_dma_start(
                        out=xs_dram, out_offset=bass.IndirectOffsetOnAxis(ap=dst_idx[:, i:i + 1], axis=0),
                        in_=rows[:, i], in_offset=None).then_inc(scat, 16)
            for q in range(2):
                pool.wait_ge(xrow_in[q], 16 * (E // 2 + 1))
                pool.wait_ge(eo_out[q], EO_COUNT * (E // 2 + 1))
            pool.wait_ge(src_rdy, 1)
            for t in range(NT):
                pool.indirect_dma_start(
                    out=rows[:, t], out_offset=None, in_=eo_dram,
                    in_offset=bass.IndirectOffsetOnAxis(ap=src_idx[:, t:t + 1], axis=0)).then_inc(gath[t], 16)
            for t in range(NT):
                pool.wait_ge(gath[t], 16)

        @block.scalar
        def _(act):
            def root(r, t):
                act.wait_ge(mv_rdy[r], t + 1)
                nc.scalar.activation(std[:, r, t:t + 1], mv[:, r, t, 1:2], ACT.Sqrt).then_inc(std_rdy[r], 1)

            for step, i in schedule:
                if step == "w_hi":
                    act.wait_ge(w_in[i], 16)
                    act.wait_ge(vec_in, 16)
                    if i < 2:
                        for k in range(KC):
                            ins = nc.scalar.activation(split_to[i][0][:, k], raw[i][:, k], ACT.Copy,
                                                       scale=vec[:, KC * i + k:KC * i + k + 1])
                    else:
                        ins = nc.scalar.activation(split_to[i][0][:], raw[i % 3][:], ACT.Copy)
                    ins.then_inc(w_hi, 1)
                elif step == "x_root":
                    root(0, i)
                elif step == "h_root":
                    root(1, i)
                elif step == "a_root":
                    root(2, i)
                elif step == "t_root":
                    root(3, i)
                elif step == "xT_hi":
                    t, b = i // 2, i % 2
                    act.wait_ge(xT_ps, t + 1)
                    if t >= 1:
                        act.wait_ge((h_mid, h_ps)[b], t)
                    nc.scalar.activation(xT[0][:, KC * b:KC * (b + 1)].rearrange("p k t -> p (k t)"),
                                         ps_x[:, b, 0:HT], ACT.Copy).then_inc(xT_hi, 1)
                elif step == "aT_hi":
                    u = i % HALF
                    act.wait_ge(aT_ps, i + 1)
                    if i >= HALF:
                        act.wait_ge(qk_ps, 2 * KC)
                        act.wait_ge(v_ps, HALF)
                    nc.scalar.activation(anT[0][:, :, u * TT:(u + 1) * TT],
                                         ps_t[:, 0:HT].rearrange("p (k t) -> p k t", k=KC), ACT.Copy).then_inc(aT_hi, 1)
                elif step == "v_copy":
                    act.wait_ge(v_ps, i + 1)
                    nc.scalar.activation(vsb[:, i], ps_p[0:TT, bank["v", i]], ACT.Copy).then_inc(v_sb, 1)
                elif step == "qk_exp":
                    act.wait_ge(qk_ps, i + 1)
                    if i == 0:
                        act.wait_ge(w_lo, 4)
                    if i >= 1:
                        act.wait_ge(qk_sb, i)
                    nc.scalar.activation(ebuf[:], ps_p[:, bank["qk", i], 0:HT], ACT.Exp).then_inc(e_sb, 1)
                elif step == "den_copy":
                    act.wait_ge(den_ps, i + 1)
                    if i >= 1:
                        act.wait_ge(qn_rdy, i)
                    nc.scalar.activation(dsb[:], ps_p[:, bank["den", i], 0:HT], ACT.Copy, bias=EPS_Z).then_inc(den_sb, 1)
                elif step == "att_hi":
                    act.wait_ge(n_ps, KC * (i + 1))
                    if i >= 1:
                        act.wait_ge(wo_ps, i)
                    nc.scalar.activation(attT[0][:].rearrange("p k t -> p (k t)"),
                                         ps_o[:, 0:HT], ACT.Copy).then_inc(att_hi, 1)
                elif step == "tT_copy":
                    act.wait_ge(tT_ps, i + 1)
                    if i >= 1:
                        act.wait_ge(g_ps, i)
                    nc.scalar.activation(t2T[:].rearrange("p k t -> p (k t)"),
                                         ps_t[:, 0:HT], ACT.Copy).then_inc(tT_sb, 1)

            def store(i, q):
                act.dma_start(eo_v[i, q, 0:P], eorow[:, q]).then_inc(eo_out[q], 16)
                for c in range(KC):
                    act.dma_start(eo_v[i, q, P:CAP, c * P:(c + 1) * P],
                                  eorest[DH * c:DH * c + REST, q]).then_inc(eo_out[q], 16)

            act.wait_ge(r_diff, 1)
            nc.scalar.activation(rt[:, 2], rt[:, 1], ACT.Exp).then_inc(r_exp, 1)
            for q in range(2):
                act.sem_inc(eo_out[q], EO_COUNT)
            with act.Fori(0, E // 2) as i:
                for q in range(2):
                    e = 2 * i + q

                    def leading(n):
                        s = q * PIECES + WP + n // 4
                        if n % 4 == 0:
                            act.wait_ge(slot_in[s], 16 * i + 16)
                        act.wait_ge(wo_used, BLOCKS * e + n + 1)
                        nc.scalar.activation(wouts[0][:, n % WB], ring[s][:, n % 4], ACT.Copy).then_inc(wo_hi, 1)

                    def hm_leading(j):
                        act.wait_ge(g_sb, WP * e + j + 1)
                        nc.scalar.activation(hms[0][:, 4 * j:4 * j + 4], hmT[:, 4 * j:4 * j + 4, 0:P],
                                             ACT.Copy).then_inc(hm_hi, 1)

                    for j in range(WP):
                        leading(j)
                        act.wait_ge(hm_ps, WP * e + j + 1)
                        nc.scalar.activation(
                            hmT[:, 4 * j:4 * j + 4].rearrange("p (b k) t -> p b (k t)", b=2),
                            ps_h[j % 2][:, :, 0:2 * CAP], ACT.Gelu).then_inc(g_sb, 1)
                        if j == 1:
                            act.wait_ge(rowT_ps, e + 1)
                            act.dma_start(xrow[:, q], xs_v[i + 1, q]).then_inc(xrow_in[q], 16)
                        if j < WP - 1:
                            hm_leading(j)
                    for n in range(WB, BLOCKS):
                        leading(n)
                        if n == WB + 2:
                            hm_leading(WP - 1)
                    act.wait_ge(eo_rdy, e + 2)
                    store(i, q)

        @block.vector
        def _(dve):
            st = Steps(dve)

            def moments(r, t, src, eps):
                n = src.shape[-1] // C
                for b in range(n):
                    ins = nc.vector.bn_stats(stats[:, r, b], src[:, b * C:(b + 1) * C])
                st.done(ins)
                st.done(nc.vector.bn_aggr(mv[:, r, t], stats[:, r, 0:n].rearrange("p a b -> p (a b)")))
                nc.vector.tensor_scalar(mv[:, r, t, 1:2], mv[:, r, t, 1:2], eps, None, ALU.add).then_inc(mv_rdy[r], 1)

            def normed(r, t, dst, src):
                dve.wait_ge(std_rdy[r], t + 1)
                st.done(nc.vector.reciprocal(rstd[:, r, t:t + 1], std[:, r, t:t + 1]))
                return nc.vector.tensor_scalar(dst, src, mv[:, r, t, 0:1], rstd[:, r, t:t + 1],
                                               ALU.subtract, ALU.mult)

            def rest(lo, src, hi):
                return nc.vector.tensor_tensor(lo, src, hi.bitcast(F32), ALU.subtract)

            dve.wait_ge(c_in, 16)
            for step, i in schedule:
                if step == "w_lo" and i < 2:
                    dve.wait_ge(w_hi, i + 1)
                    dve.wait_ge(vec_in, 16)
                    for k in range(KC):
                        ins = nc.vector.scalar_tensor_tensor(
                            split_to[i][1][:, k], raw[i][:, k], vec[:, KC * i + k:KC * i + k + 1],
                            split_to[i][0][:, k].bitcast(F32), ALU.mult, ALU.subtract)
                    ins.then_inc(wt_lo, 1)
                elif step == "bias_add":
                    dve.wait_ge(bias_ps, 1)
                    dve.wait_ge(bcst_in, 16)
                    nc.vector.tensor_tensor(bcst[:, 2], bcst[:, 2], ps_p[0:TT, bank["bias", 0]], ALU.add).then_inc(bias_sb, 1)
                elif step == "x_stats":
                    dve.wait_ge(x_in[i % 2], 16 * (i // 2 + 1))
                    moments(0, i, xt[:, i % 2], EPS_TOK)
                elif step == "x_norm":
                    normed(0, i, xt[:, i % 2], xt[:, i % 2]).then_inc(x_norm, 1)
                elif step == "xT_lo":
                    dve.wait_ge(xT_hi, i + 1)
                    part = [w[:, KC * (i % 2):KC * (i % 2 + 1)].rearrange("p k t -> p (k t)") for w in xT]
                    rest(part[1], ps_x[:, i % 2, 0:HT], part[0]).then_inc(xT_lo, 1)
                elif step == "h_stats":
                    dve.wait_ge(h_ps, i + 1)
                    if i == NT - 2:
                        dve.wait_ge(z_out, 16 * (E + 3))
                    if i == 0:
                        dve.wait_ge(bias_sb, 1)
                    nc.vector.tensor_tensor(h2[:, i], ps_p[0:TT, bank["embed", i]], bcst[:, 2], ALU.add).then_inc(h_evac, 1)
                    dve.wait_ge(h_evac, i + 1)
                    moments(1, i, h2[:, i], EPS_TOK)
                elif step == "h_norm":
                    normed(1, i, h2[:, i], h2[:, i]).then_inc(h_norm, 1)
                elif step == "a_stats":
                    dve.wait_ge(h_rdy, i + 1)
                    moments(2, i, h2[:, i], EPS_LN)
                elif step == "a_norm":
                    if i >= 1:
                        dve.wait_ge(aT_ps, i)
                    normed(2, i, an[:], h2[:, i]).then_inc(a_norm, 1)
                elif step == "aT_lo":
                    u = i % HALF
                    dve.wait_ge(aT_hi, i + 1)
                    part = [w[:, :, u * TT:(u + 1) * TT] for w in anT]
                    rest(part[1], ps_t[:, 0:HT].rearrange("p (k t) -> p k t", k=KC), part[0]).then_inc(aT_lo, 1)
                elif step == "qk_elu":
                    dve.wait_ge(e_sb, i + 1)
                    st.done(nc.vector.tensor_scalar(ebuf[:], ebuf[:], 1.0, None, ALU.min))
                    if i == 2 * KC:
                        dve.wait_ge(h_ps, NT)
                    dst = (kTs if i % 2 == 0 else qTs)[i // (2 * KC)][:, i // 2 % KC]
                    nc.vector.scalar_tensor_tensor(dst, ps_p[:, bank["qk", i], 0:HT], 0.0, ebuf[:],
                                                   ALU.max, ALU.add).then_inc(qk_sb, 1)
                elif step == "q_times_sum":
                    g, m = i // KC, i % KC
                    per = lambda a: a.rearrange("p (b s) -> p b s", s=NPATCH)
                    dve.wait_ge(qk_sb, 2 * i + 2)
                    st.done(nc.vector.reduce_sum(ksum[:], per(kTs[g][:, m]), AX_X))
                    if i >= 1:
                        dve.wait_ge(den_ps, i)
                    nc.vector.tensor_tensor(per(kq[:]), per(qTs[g][:, m]),
                                            ksum[:].unsqueeze(2).to_broadcast([P, HT // NPATCH, NPATCH]),
                                            ALU.mult).then_inc(kq_rdy, 1)
                elif step == "den_inv":
                    dve.wait_ge(den_sb, i + 1)
                    nc.vector.reciprocal(dsb[:], dsb[:]).then_inc(den_inv, 1)
                elif step == "mask":
                    dve.wait_ge(s_ps, i + 1)
                    if i >= 2:
                        dve.wait_ge(n_ps, i - 1)
                    mask = cst[0:TT, CO_MASK:CO_MASK + TT].unsqueeze(1).to_broadcast([TT, HPB, TT])
                    nc.vector.tensor_tensor(ssb[:, i % 2].rearrange("p (h t) -> p h t", h=HPB),
                                            ps_s[0:TT, i % 2, 0:HPB * TT].rearrange("p (h t) -> p h t", h=HPB),
                                            mask, ALU.mult).then_inc(s_sb, 1)
                elif step == "att_lo":
                    dve.wait_ge(att_hi, i + 1)
                    rest(attT[1][:].rearrange("p k t -> p (k t)"), ps_o[:, 0:HT],
                         attT[0][:].rearrange("p k t -> p (k t)")).then_inc(att_lo, 1)
                elif step == "residual":
                    dve.wait_ge(wo_ps, i + 1)
                    nc.vector.tensor_tensor(h2[:, i], h2[:, i], ps_p[0:TT, bank["project", i]], ALU.add).then_inc(h2_rdy, 1)
                    dve.wait_ge(h2_rdy, i + 1)
                    moments(3, i, h2[:, i], EPS_LN)
                elif step == "t_norm":
                    if i >= 1:
                        dve.wait_ge(tT_ps, i)
                    normed(3, i, tn[:], h2[:, i]).then_inc(t_norm, 1)
                elif step == "gate_copy":
                    dve.wait_ge(g_ps, i + 1)
                    nc.vector.tensor_copy(logits[:, i], ps_p[0:TT, bank["gate", i], 0:E]).then_inc(lg_sb, 1)
                elif step == "pick":
                    first, end = GROUPS[i]
                    r0, r1, r2 = (rt[:, n, E * first:E * end] for n in range(3))
                    by_expert = lambda a: a.rearrange("p (t e) -> p t e", e=E)
                    per_e = lambda a: a.unsqueeze(2).to_broadcast([TT, end - first, E])
                    top, rev = rs[:, 0, first:end], rs[:, 1, first:end]
                    dve.wait_ge(lg_sb, end)
                    if i == 0:
                        nc.vector.tensor_copy(trib[:, 0:TT], cst[0:TT, CO_TRI:CO_TRI + TT])
                        nc.vector.memset(trib[:, TT:2 * TT], 1.0)
                    st.done(nc.vector.reduce_max(top, logits[:, first:end], AX_X))
                    st.done(nc.vector.tensor_tensor(by_expert(r1), logits[:, first:end], per_e(top), ALU.is_equal))
                    st.done(nc.vector.tensor_tensor(r2, r1, cst[0:TT, CO_REV:CO_REV + E * (end - first)], ALU.mult))
                    st.done(nc.vector.reduce_max(rev, by_expert(r2), AX_X))
                    st.done(nc.vector.tensor_tensor(by_expert(r0), by_expert(r2), per_e(rev), ALU.is_equal))
                    nc.vector.tensor_copy(ohb[:, E * first:E * end], r0).then_inc(r_oh, 1)
                elif step == "place":
                    first, end = GROUPS[i]
                    r0, r1, r2 = (rt[:, n, E * first:E * end] for n in range(3))
                    by_expert = lambda a: a.rearrange("p (t e) -> p t e", e=E)
                    base, rank, kept, slot = (rs[:, n, first:end] for n in range(2, 6))
                    spare = rs[:, 1, first:end]
                    own = cst[0:TT, CO_TOK + first:CO_TOK + end]
                    st.done(nc.vector.tensor_tensor(r1, r0, cst[0:TT, CO_OFF:CO_OFF + E * (end - first)], ALU.mult))
                    st.done(nc.vector.reduce_sum(base, by_expert(r1), AX_X))
                    dve.wait_ge(r_ps, i + 1)
                    if end == NT:
                        nc.vector.tensor_copy(counts[:], ps_p[0:1, bank["rank", i], NT * E:(NT + 1) * E]).then_inc(counts_rdy, 1)
                    nc.vector.tensor_tensor(r2, r0, ps_p[0:TT, bank["rank", i], E * first:E * end],
                                            ALU.mult).then_inc(rank_read, 1)
                    dve.wait_ge(rank_read, i + 1)
                    st.done(nc.vector.reduce_sum(rank, by_expert(r2), AX_X))
                    st.done(nc.vector.tensor_tensor(slot, rank, base, ALU.add))
                    st.done(nc.vector.tensor_tensor(spare, slot, own, ALU.subtract))
                    st.done(nc.vector.scalar_tensor_tensor(base, rank, float(CAP), spare, ALU.is_lt, ALU.mult))
                    nc.vector.tensor_tensor(dst_idx[:, first:end], base, own, ALU.add).then_inc(idx_rdy, 1)
                    nc.vector.tensor_scalar(kept, rank, float(CAP), None, ALU.is_lt)
                elif step == "row":
                    if i == 0:
                        dve.wait_ge(aT_ps, NT)
                    nc.vector.tensor_scalar(rows[:, i], h2[:, i], mv[:, 3, i, 0:1], rstd[:, 3, i:i + 1],
                                            ALU.subtract, ALU.mult).then_inc(rows_rdy, 1)

            dve.wait_ge(idx_rdy, len(GROUPS))
            st.done(nc.vector.tensor_scalar(rs[:, 1], rs[:, 5], 1.0, None, ALU.add))
            st.done(nc.vector.tensor_tensor(rs[:, 2], rs[:, 1], rs[:, 4], ALU.mult))
            nc.vector.tensor_copy(src_idx[:], rs[:, 2]).then_inc(src_rdy, 1)
            t3 = [rt[:, n].rearrange("p (t e) -> p t e", e=E) for n in range(3)]
            nc.vector.tensor_tensor(t3[1], logits[:], rs[:, 0].unsqueeze(2).to_broadcast([TT, NT, E]),
                                    ALU.subtract).then_inc(r_diff, 1)
            dve.wait_ge(r_exp, 1)
            st.done(nc.vector.reduce_sum(rs[:, 1], t3[2], AX_X))
            st.done(nc.vector.reciprocal(rs[:, 2], rs[:, 1]))
            nc.vector.tensor_tensor(prob[:], rs[:, 2], rs[:, 4], ALU.mult)

            dve.wait_ge(rowT_ps, 1)
            nc.vector.tensor_copy(xTe[:, 0].rearrange("p (b k) t -> p b (k t)", b=2),
                                  ps_s[:, :, 0:2 * CAP]).then_inc(rowT_sb, 1)
            dve.sem_inc(eo_rdy, 1)
            with dve.Fori(0, E // 2) as i:
                for q in range(2):
                    e = 2 * i + q

                    def trailing(n):
                        dve.wait_ge(wo_hi, BLOCKS * e + n + 1)
                        rest(wouts[1][:, n % WB], ring[q * PIECES + WP + n // 4][:, n % 4],
                             wouts[0][:, n % WB]).then_inc(wo_lo, 1)

                    def hm_trailing(j):
                        dve.wait_ge(hm_hi, WP * e + j + 1)
                        part = [w[:, 4 * j:4 * j + 4] for w in hms]
                        rest(part[1], hmT[:, 4 * j:4 * j + 4, 0:P], part[0]).then_inc(hm_lo, 1)

                    for j in range(WP):
                        trailing(j)
                        if j < WP - 1:
                            hm_trailing(j)
                        if j == 1:
                            dve.wait_ge(rowT_ps, e + 2)
                            nc.vector.tensor_copy(xTe[:, 1 - q].rearrange("p (b k) t -> p b (k t)", b=2),
                                                  ps_s[:, :, 0:2 * CAP]).then_inc(rowT_sb, 1)
                    for n in range(WB, BLOCKS):
                        trailing(n)
                        if n == WB + 2:
                            hm_trailing(WP - 1)
                    dve.wait_ge(wo_used, BLOCKS * (e + 1) + WB)
                    dve.wait_ge(eo_out[q], EO_COUNT * (i + 1))
                    nc.vector.tensor_copy(eorest[:, q], ps_o[:, 0:P])
                    nc.vector.tensor_copy(eorow[:, q], ps_t[:]).then_inc(eo_rdy, 1)
            for t in range(NT):
                dve.wait_ge(gath[t], 16)
                nc.vector.scalar_tensor_tensor(h2[:, t], rows[:, t], prob[:, t:t + 1], h2[:, t],
                                               ALU.mult, ALU.add).then_inc(o_rdy, 1)

        @block.tensor
        def _(pe):
            def mm(o, a, b, first, last, **kw):
                return nc.tensor.matmul(o, a, b, start=first, stop=last, **kw)

            def mm3(o, a, b, first, last):
                mm(o, a[0], b[0], first, False)
                mm(o, a[0], b[1], False, False)
                return mm(o, a[1], b[0], False, last)

            def of(pair, *at_):
                return [w[at_] for w in pair]

            def free(table, key):
                if table[key]:
                    pe.wait_ge(*table[key])

            every = slice(None)
            pe.wait_ge(c_in, 16)
            for step, i in schedule:
                if step == "bias":
                    pe.wait_ge(w_in[0], 16)
                    pe.wait_ge(w_in[1], 16)
                    pe.wait_ge(vec_in, 16)
                    for k in range(KX):
                        ins = mm(ps_p[0:TT, bank[step, i]], vec[:, KX + k:KX + k + 1].to_broadcast([P, TT]),
                                 raw[k // KC][:, k % KC], k == 0, k == KX - 1)
                    ins.then_inc(bias_ps, 1)
                elif step == "x_turn":
                    pe.wait_ge(x_norm, i + 1)
                    if i >= 1:
                        pe.wait_ge(xT_lo, 2 * i)
                    for k in range(KX):
                        ins = nc.tensor.transpose(ps_x[:, k // 4, (k % 4) * TT:(k % 4 + 1) * TT],
                                                  xt[:, i % 2, k * P:(k + 1) * P], ident[0:TT, 0:TT])
                    ins.then_inc(xT_ps, 1)
                elif step == "embed":
                    if i == 0:
                        pe.wait_ge(wt_lo, 2)
                    free(before, (step, i))
                    for b, done in enumerate((h_mid, h_ps)):
                        pe.wait_ge(xT_lo, 2 * i + b + 1)
                        for k in range(KC * b, KC * (b + 1)):
                            ins = mm3(ps_p[0:TT, bank[step, i]], of(xT, every, k), of(wtok, every, k), k == 0, k == KX - 1)
                        ins.then_inc(done, 1)
                elif step == "a_turn":
                    pe.wait_ge(a_norm, i + 1)
                    free(before_t, (step, i))
                    for k in range(KC):
                        ins = nc.tensor.transpose(ps_t[:, k * TT:(k + 1) * TT], an[:, k * P:(k + 1) * P], ident[0:TT, 0:TT])
                    ins.then_inc(aT_ps, 1)
                elif step == "v":
                    u = i % HALF
                    pe.wait_ge(aT_lo, i + 1)
                    if i == 0:
                        pe.wait_ge(w_lo, 1)
                    free(before, (step, i))
                    for k in range(KC):
                        ins = mm3(ps_p[0:TT, bank[step, i]], of(anT, every, k, slice(u * TT, (u + 1) * TT)),
                                  of(wvs, every, k), k == 0, k == KC - 1)
                    ins.then_inc(v_ps, 1)
                elif step == "qk":
                    w, m = (wks, wqs)[i % 2], i // 2 % KC
                    if i % (2 * KC) == 0:
                        pe.wait_ge(aT_lo, HALF * (i // (2 * KC) + 1))
                        pe.wait_ge(w_lo, 3)
                    free(before, (step, i))
                    for k in range(KC):
                        ins = mm3(ps_p[:, bank[step, i], 0:HT], of(w, every, k, slice(m * P, (m + 1) * P)),
                                  of(anT, every, k), k == 0, k == KC - 1)
                    ins.then_inc(qk_ps, 1)
                elif step == "den":
                    pe.wait_ge(kq_rdy, i + 1)
                    free(before, (step, i))
                    mm(ps_p[:, bank[step, i], 0:HT], cst[:, CO_BLK:CO_BLK + P], kq[:], True, True).then_inc(den_ps, 1)
                elif step == "scores":
                    u, m = i // KC % HALF, i % KC
                    pe.wait_ge(qb_rdy, i + 1)
                    if i >= 2:
                        pe.wait_ge(s_sb, i - 1)
                    mm(ps_s[0:TT, i % 2, 0:HPB * TT], kTs[i // (HALF * KC)][:, m, u * TT:(u + 1) * TT], qblk[:, i % 2],
                       True, True).then_inc(s_ps, 1)
                elif step == "attend":
                    u, m = i // KC % HALF, i % KC
                    pe.wait_ge(s_sb, i + 1)
                    if m == 0:
                        pe.wait_ge(v_sb, i // KC + 1)
                    if m == 0 and i >= KC:
                        pe.wait_ge(att_lo, i // KC)
                    for h in range(HPB):
                        ins = mm(ps_o[DH * h:DH * (h + 1), m * TT:(m + 1) * TT],
                                 vsb[:, i // KC, m * P + DH * h:m * P + DH * (h + 1)],
                                 ssb[:, i % 2, h * TT:(h + 1) * TT], True, True)
                    ins.then_inc(n_ps, 1)
                elif step == "project":
                    pe.wait_ge(att_lo, i + 1)
                    if i == 0:
                        pe.wait_ge(w_lo, 4)
                    free(before, (step, i))
                    for k in range(KC):
                        ins = mm3(ps_p[0:TT, bank[step, i]], of(attT, every, k), of(wos, every, k), k == 0, k == KC - 1)
                    ins.then_inc(wo_ps, 1)
                elif step == "t_turn":
                    pe.wait_ge(t_norm, i + 1)
                    free(before_t, (step, i))
                    for k in range(KC):
                        ins = nc.tensor.transpose(ps_t[:, k * TT:(k + 1) * TT], tn[:, k * P:(k + 1) * P], ident[0:TT, 0:TT])
                    ins.then_inc(tT_ps, 1)
                elif step == "gate":
                    pe.wait_ge(tT_sb, i + 1)
                    if i == 0:
                        pe.wait_ge(gate_in, 16)
                    free(before, (step, i))
                    for k in range(KC):
                        ins = mm(ps_p[0:TT, bank[step, i], 0:E], t2T[:, k], gsb[:, k], k == 0, k == KC - 1)
                    ins.then_inc(g_ps, 1)
                elif step == "rank":
                    first, end = GROUPS[i]
                    pe.wait_ge(r_oh, i + 1)
                    free(before, (step, i))
                    to = end + 1 if end == NT else end
                    for d in range(to):
                        a, b = max(first, d), end if d == 0 else to
                        ins = mm(ps_p[0:TT, bank[step, i], E * a:E * b], trib[:, TT * min(d, 1):TT * (min(d, 1) + 1)],
                                 ohb[:, E * (a - d):E * (b - d)], d == 0, d == to - 1, skip_group_check=True)
                    ins.then_inc(r_ps, 1)

            def slots_turned(e, q):
                pe.wait_ge(xrow_in[q], 8 * (e - q) + 16)
                for k in range(KC):
                    for c in range(2):
                        ins = nc.tensor.transpose(
                            ps_s[:, k // 2, (k % 2) * CAP + c * CH:(k % 2) * CAP + (c + 1) * CH],
                            xrow[:, q, c, k * P:(k + 1) * P], ident[0:CH, 0:CH])
                ins.then_inc(rowT_ps, 1)

            def expert(i, q, width):
                e = 2 * i + q
                for j in range(WP):
                    s = q * PIECES + j
                    pe.wait_ge(slot_in[s], 16 * i + 16)
                    if j == 0:
                        pe.wait_ge(rowT_sb, e + 1)
                    if j >= 2:
                        pe.wait_ge(g_sb, WP * e + j - 1)
                    for c in range(4):
                        for k in range(KC):
                            ins = mm(ps_h[j % 2][:, c // 2, (c % 2) * CAP:(c % 2) * CAP + width],
                                     ring[s][:, k, c * P:(c + 1) * P], xTe[:, q, k, 0:width], k == 0, k == KC - 1)
                    ins.then_inc(hm_ps, 1)
                    if j == 1:
                        slots_turned(e + 1, 1 - q)
                for j in range(WP):
                    s = q * PIECES + WP + j
                    if j == 0:
                        pe.wait_ge(eo_rdy, e + 1)
                    pe.wait_ge(slot_in[s], 16 * i + 16)
                    pe.wait_ge(hm_lo, WP * e + j + 1)
                    if width > P:
                        for b in range(4):
                            for c in range(KC):
                                mm(ps_o[DH * c:DH * c + REST, 0:P], hmT[:, 4 * j + b, P:CAP],
                                   ring[s][:, b, c * P:(c + 1) * P], j == 0 and b == 0, j == WP - 1 and b == 3)
                    for b in range(4):
                        n = 4 * j + b
                        pe.wait_ge(wo_lo, BLOCKS * e + n + 1)
                        ins = mm3(ps_t[:], of(hms, every, n), of(wouts, every, n % WB), n == 0, n == BLOCKS - 1)
                        ins.then_inc(wo_used, 1)
                pe.wait_ge(rowT_sb, e + 2)

            pe.sem_inc(wo_used, WB)
            slots_turned(0, 0)
            pe.wait_ge(counts_rdy, 1)
            with pe.Fori(0, E // 2) as i:
                for q in range(2):
                    tokens = pe.value_load(counts[0:1, bass.ds(2 * i + q, 1)], min_val=0, max_val=TOKENS)
                    with pe.If(tokens < P + 1):
                        expert(i, q, P)
                    with pe.Else():
                        expert(i, q, CAP)


def kernel(x, L0_tok_W, L0_tok_b, L0_tok_g1, L0_tok_b1, L0_tok_g2, L0_tok_b2, L0_attn_cos, L0_attn_sin,
           L0_attn_Wq, L0_attn_Wk, L0_attn_Wv, L0_attn_Wo, L0_ffn_gate_weight, L0_ffn_wi, L0_ffn_wo):
    import concourse.bacc as bacc
    from concourse.bass_utils import run_bass_kernel_spmd

    a = np.asarray
    t = lambda w: np.ascontiguousarray(a(w).T)
    by_partition = lambda v: a(v).reshape(KX, P).T
    ins = {
        "x": np.ascontiguousarray(a(x)[:, :NPATCH * TIN]).reshape(TOKENS, IN_DIM),
        "w_tok": a(L0_tok_W),
        "cols": np.ascontiguousarray(np.concatenate([by_partition(L0_tok_g1), by_partition(L0_tok_b1)], 1)),
        "g2b2b": np.stack([a(L0_tok_g2), a(L0_tok_b2), a(L0_tok_b)]),
        "wq": t(L0_attn_Wq), "wk": t(L0_attn_Wk), "wv": t(L0_attn_Wv), "wo": t(L0_attn_Wo),
        "gate": t(L0_ffn_gate_weight),
        "wi": a(L0_ffn_wi), "wout": a(L0_ffn_wo),
        "consts": constants(),
    }
    nc = bacc.Bacc("TRN2", target_bir_lowering=False, num_devices=1)
    args = {n: nc.dram_tensor(f"in_{n}", v.shape, F32, kind="ExternalInput").ap() for n, v in ins.items()}
    args["out"] = nc.dram_tensor("out_0", (TOKENS, C), F32, kind="ExternalOutput").ap()
    audio_tower(nc, **args)
    r = run_bass_kernel_spmd(nc, [{f"in_{n}": v for n, v in ins.items()}], core_ids=[0])
    return r.results[0]["out_0"].reshape(BATCH, NPATCH, C)
```
